# Optimizing a Trainium2 kernel written in Bass

```python
import numpy as np
import jax
import jax.numpy as jnp

def _softmax(x, axis=-1):
    return jax.nn.softmax(x, axis=axis)

def _gelu(x):
    return jax.nn.gelu(x, approximate=True)

def _silu(x):
    return jax.nn.silu(x)

def _sigmoid(x):
    return jax.nn.sigmoid(x)

def _layernorm(x, axis=-1, eps=1e-05):
    m = jnp.mean(x, axis=axis, keepdims=True)
    v = jnp.var(x, axis=axis, keepdims=True)
    return (x - m) / jnp.sqrt(v + eps)

def _scatter_add(tgt, idx, src, axis=0):
    return tgt.at[idx].add(src)

def _segment_sum(src, seg, n):
    return jax.ops.segment_sum(src, seg, n)
kernel_name = 'mk_rec_standalone_d1_rec_r8_6722cf'

def setup_inputs(seed: int=0):
    np.random.seed(seed)
    _w = jnp.asarray

    def _rec_inputs():
        import jax
        import jax.numpy as jnp
        _rk = jax.random.key(seed)
        r_num_features = -0.00338568 + 1.0005 * jax.random.normal(jax.random.fold_in(_rk, 1), (2048, 13), jnp.float32)
        r_cat_features = jnp.stack([jax.random.randint(jax.random.fold_in(jax.random.fold_in(_rk, 2), 0), (2048,), 0, 1250, jnp.int32), jax.random.randint(jax.random.fold_in(jax.random.fold_in(_rk, 2), 1), (2048,), 0, 1250, jnp.int32), jax.random.randint(jax.random.fold_in(jax.random.fold_in(_rk, 2), 2), (2048,), 0, 1250, jnp.int32), jax.random.randint(jax.random.fold_in(jax.random.fold_in(_rk, 2), 3), (2048,), 0, 1250, jnp.int32), jax.random.randint(jax.random.fold_in(jax.random.fold_in(_rk, 2), 4), (2048,), 0, 1250, jnp.int32), jax.random.randint(jax.random.fold_in(jax.random.fold_in(_rk, 2), 5), (2048,), 0, 1250, jnp.int32), jax.random.randint(jax.random.fold_in(jax.random.fold_in(_rk, 2), 6), (2048,), 0, 1250, jnp.int32), jax.random.randint(jax.random.fold_in(jax.random.fold_in(_rk, 2), 7), (2048,), 0, 1250, jnp.int32), jax.random.randint(jax.random.fold_in(jax.random.fold_in(_rk, 2), 8), (2048,), 0, 1250, jnp.int32), jax.random.randint(jax.random.fold_in(jax.random.fold_in(_rk, 2), 9), (2048,), 1, 1250, jnp.int32), jax.random.randint(jax.random.fold_in(jax.random.fold_in(_rk, 2), 10), (2048,), 1, 9999, jnp.int32), jax.random.randint(jax.random.fold_in(jax.random.fold_in(_rk, 2), 11), (2048,), 0, 1250, jnp.int32), jax.random.randint(jax.random.fold_in(jax.random.fold_in(_rk, 2), 12), (2048,), 0, 1250, jnp.int32), jax.random.randint(jax.random.fold_in(jax.random.fold_in(_rk, 2), 13), (2048,), 0, 9999, jnp.int32), jax.random.randint(jax.random.fold_in(jax.random.fold_in(_rk, 2), 14), (2048,), 0, 1250, jnp.int32), jax.random.randint(jax.random.fold_in(jax.random.fold_in(_rk, 2), 15), (2048,), 0, 1250, jnp.int32), jax.random.randint(jax.random.fold_in(jax.random.fold_in(_rk, 2), 16), (2048,), 1, 1250, jnp.int32), jax.random.randint(jax.random.fold_in(jax.random.fold_in(_rk, 2), 17), (2048,), 0, 1250, jnp.int32), jax.random.randint(jax.random.fold_in(jax.random.fold_in(_rk, 2), 18), (2048,), 1, 1250, jnp.int32), jax.random.randint(jax.random.fold_in(jax.random.fold_in(_rk, 2), 19), (2048,), 0, 1250, jnp.int32), jax.random.randint(jax.random.fold_in(jax.random.fold_in(_rk, 2), 20), (2048,), 0, 1250, jnp.int32), jax.random.randint(jax.random.fold_in(jax.random.fold_in(_rk, 2), 21), (2048,), 1, 1250, jnp.int32), jax.random.randint(jax.random.fold_in(jax.random.fold_in(_rk, 2), 22), (2048,), 0, 1250, jnp.int32), jax.random.randint(jax.random.fold_in(jax.random.fold_in(_rk, 2), 23), (2048,), 1, 1250, jnp.int32), jax.random.randint(jax.random.fold_in(jax.random.fold_in(_rk, 2), 24), (2048,), 2, 1250, jnp.int32), jax.random.randint(jax.random.fold_in(jax.random.fold_in(_rk, 2), 25), (2048,), 1, 1250, jnp.int32)], axis=1)
        return (r_num_features, r_cat_features)
    r_num_features, r_cat_features = _rec_inputs()

    def _L0_rec_setup():
        import jax, jax.numpy as jnp
        import numpy as np
        B, NUM_NUM, NUM_CAT, VOCAB = (2048, 13, 26, 1250)
        E, L, H = (64, 3, 2)
        F = NUM_NUM + NUM_CAT
        D = E // H

        def _interact(x, wq, wk, wv, wo, wres):
            b, f, e = x.shape
            Q = (x @ wq.T).reshape(b, f, H, D)
            K = (x @ wk.T).reshape(b, f, H, D)
            V = (x @ wv.T).reshape(b, f, H, D)
            scores = jnp.einsum('bqhd,bkhd->bhqk', Q, K) / jnp.sqrt(jnp.float32(D))
            attn = jax.nn.softmax(scores, axis=-1)
            out = jnp.einsum('bhqk,bkhd->bqhd', attn, V).reshape(b, f, e)
            return out @ wo.T + x @ wres.T
        key = jax.random.key(seed)
        ks = jax.random.split(key, 12)
        s = 0.05
        return {'num_features': jax.random.normal(ks[0], (B, NUM_NUM), dtype=jnp.float32), 'cat_features': jax.random.randint(ks[1], (B, NUM_CAT), 0, VOCAB), 'W_num': jax.random.normal(ks[2], (NUM_NUM, E), dtype=jnp.float32) * s, 'b_num': jax.random.normal(ks[3], (NUM_NUM, E), dtype=jnp.float32) * s, 'cat_tables': jax.random.normal(ks[4], (NUM_CAT, VOCAB, E), dtype=jnp.float32) * s, 'W_Q': jax.random.normal(ks[5], (L, E, E), dtype=jnp.float32) * s, 'W_K': jax.random.normal(ks[6], (L, E, E), dtype=jnp.float32) * s, 'W_V': jax.random.normal(ks[7], (L, E, E), dtype=jnp.float32) * s, 'W_O': jax.random.normal(ks[8], (L, E, E), dtype=jnp.float32) * s, 'W_Res': jax.random.normal(ks[9], (L, E, E), dtype=jnp.float32) * s, 'W_final': jax.random.normal(ks[10], (1, F * E), dtype=jnp.float32) * s, 'b_final': jax.random.normal(ks[11], (1,), dtype=jnp.float32) * s}
    _L0_rec_all = _L0_rec_setup()
    _L0_rec_in = {k: v for k, v in _L0_rec_all.items() if k in ('W_num', 'b_num', 'cat_tables', 'W_Q', 'W_K', 'W_V', 'W_O', 'W_Res', 'W_final', 'b_final')}
    del _L0_rec_all
    return {'r_num_features': r_num_features, 'r_cat_features': r_cat_features, 'L0_rec_W_num': _L0_rec_in['W_num'], 'L0_rec_b_num': _L0_rec_in['b_num'], 'L0_rec_cat_tables': _L0_rec_in['cat_tables'], 'L0_rec_W_Q': _L0_rec_in['W_Q'], 'L0_rec_W_K': _L0_rec_in['W_K'], 'L0_rec_W_V': _L0_rec_in['W_V'], 'L0_rec_W_O': _L0_rec_in['W_O'], 'L0_rec_W_Res': _L0_rec_in['W_Res'], 'L0_rec_W_final': _L0_rec_in['W_final'], 'L0_rec_b_final': _L0_rec_in['b_final']}

def reference(r_num_features, r_cat_features, L0_rec_W_num, L0_rec_b_num, L0_rec_cat_tables, L0_rec_W_Q, L0_rec_W_K, L0_rec_W_V, L0_rec_W_O, L0_rec_W_Res, L0_rec_W_final, L0_rec_b_final):
    import jax
    import jax.numpy as jnp

    def _L0_rec_ref(num_features, cat_features, W_num, b_num, cat_tables, W_Q, W_K, W_V, W_O, W_Res, W_final, b_final):
        import jax, jax.numpy as jnp
        import numpy as np
        B, NUM_NUM, NUM_CAT, VOCAB = (2048, 13, 26, 1250)
        E, L, H = (64, 3, 2)
        F = NUM_NUM + NUM_CAT
        D = E // H

        def _interact(x, wq, wk, wv, wo, wres):
            b, f, e = x.shape
            Q = (x @ wq.T).reshape(b, f, H, D)
            K = (x @ wk.T).reshape(b, f, H, D)
            V = (x @ wv.T).reshape(b, f, H, D)
            scores = jnp.einsum('bqhd,bkhd->bhqk', Q, K) / jnp.sqrt(jnp.float32(D))
            attn = jax.nn.softmax(scores, axis=-1)
            out = jnp.einsum('bhqk,bkhd->bqhd', attn, V).reshape(b, f, e)
            return out @ wo.T + x @ wres.T
        num_emb = num_features[:, :, None] * W_num[None] + b_num[None]
        cat_emb = cat_tables[jnp.arange(NUM_CAT), cat_features]
        x = jnp.concatenate([num_emb, cat_emb], axis=1)
        for l in range(L):
            x = _interact(x, W_Q[l], W_K[l], W_V[l], W_O[l], W_Res[l])
        flat = x.reshape(x.shape[0], -1)
        logits = flat @ W_final.T + b_final
        return jax.nn.sigmoid(logits.squeeze(-1))
    y = _L0_rec_ref(r_num_features, r_cat_features, L0_rec_W_num, L0_rec_b_num, L0_rec_cat_tables, L0_rec_W_Q, L0_rec_W_K, L0_rec_W_V, L0_rec_W_O, L0_rec_W_Res, L0_rec_W_final, L0_rec_b_final)
    return y

_drawn_inputs = setup_inputs


def setup_inputs(seed=0):
    import zlib

    import numpy as np

    out = dict(_drawn_inputs(seed))
    spreads = {}
    factors = {'r_num_features': 8.0,
     'L0_rec_W_num': 8.0,
     'L0_rec_b_num': 8.0,
     'L0_rec_cat_tables': 8.0,
     'L0_rec_W_Q': 8.0,
     'L0_rec_W_K': 8.0,
     'L0_rec_W_V': 8.0,
     'L0_rec_W_O': 8.0,
     'L0_rec_W_Res': 8.0,
     'L0_rec_W_final': 8.0}
    for name, (base, spread) in spreads.items():
        noise = np.random.default_rng([zlib.crc32(name.encode()), seed]).standard_normal(out[name].shape)
        drawn = base * np.exp(spread * noise) if base else spread * noise
        out[name] = jnp.asarray(drawn.astype(out[name].dtype))
    for name, factor in factors.items():
        out[name] = (out[name] * factor).astype(out[name].dtype)
    return out
```

```python
from contextlib import ExitStack

import concourse.bass as bass
from concourse import mybir

F32 = mybir.dt.float32
I32 = mybir.dt.int32
U32 = mybir.dt.uint32
ALU = mybir.AluOpType
ACT = mybir.ActivationFunctionType
AX = mybir.AxisListType.X

B, NUM_NUM, NUM_CAT, VOCAB = 2048, 13, 26, 1250
E, L, H = 64, 3, 2
F = NUM_NUM + NUM_CAT
D = E // H

J = 3
T = 2
G = 2
TOK = J * F
CH = G * T * J
CHUNKS = -(-B // CH)
STEPS = CHUNKS + 1
NT = G * T
COLS = (CHUNKS + 2) * NT
CAT_ROWS = J * NUM_CAT
NUM_ROWS = J * NUM_NUM
P = 128
SCALE = float(D) ** -0.5

WINDOWS = ((0, 1), (2, 0), (1, 2))
W = len(WINDOWS)


def recsys_attention(nc, num, cat, cat_base, w_num, b_num, tables, wq, wk, wv, wo_t, wres_t, w_fin, b_fin, out):
    with ExitStack() as ctx:
        def sb(name, shape, dt=F32):
            return ctx.enter_context(nc.sbuf_tensor(name, shape, dt))

        def bank(name):
            return ctx.enter_context(nc.psum_tensor(name, [P, 512], F32))

        def sem(name):
            return ctx.enter_context(nc.semaphore(name))

        wq_sb = sb("wq_sb", [E, L, E])
        wk_sb = sb("wk_sb", [E, L, T, E])
        wv_sb = sb("wv_sb", [E, L, T, E])
        wo_sb = sb("wo_sb", [E, L, E])
        key_w = sb("key_w", [P, L, H, T, E])
        val_w = sb("val_w", [P, L, H, E])
        res_w = sb("res_w", [P, L, T, E])
        fin_w = sb("fin_w", [P, F])
        fin_b = sb("fin_b", [T, 1])
        num_w = sb("num_w", [NUM_ROWS, E])
        num_b = sb("num_b", [NUM_ROWS, E])
        ident = sb("ident", [P, P])
        same = sb("same", [P, J])
        halves = sb("halves", [P, T])
        cat_sb = sb("cat_sb", [CAT_ROWS, COLS], I32)
        base_sb = sb("base_sb", [CAT_ROWS, 1], I32)
        cat_f = sb("cat_f", [CAT_ROWS, COLS])
        neg_f = sb("neg_f", [CAT_ROWS, COLS])
        base_f = sb("base_f", [CAT_ROWS, 1])
        row_sb = sb("row_sb", [CAT_ROWS, COLS], U32)
        num_sb = sb("num_sb", [NUM_ROWS, COLS])
        rows_now = sb("rows_now", [CAT_ROWS, NT], U32)
        tok_cat = sb("tok_cat", [CAT_ROWS, G, T, E])
        tok_num = sb("tok_num", [NUM_ROWS, G, T, E])
        tok_mul = sb("tok_mul", [NUM_ROWS, G, T, E])
        xt = [sb(f"xt{n}", [P, G, TOK]) for n in range(L)]
        keys = sb("keys", [P, G, J, H, F])
        vals = [sb(f"vals{n}", [TOK, G, T, H, E]) for n in range(L)]
        probs = sb("probs", [P, G, H, J, F])
        top = sb("top", [P, G, J, H])
        den = sb("den", [P, G, H, J])
        inv = sb("inv", [P, G, H, J])
        mix = sb("mix", [TOK, G * H * T, J, F])
        fin_x = sb("fin_x", [P, G, J, F])
        partial = sb("partial", [P, STEPS, G * J])
        z = sb("z", [T, STEPS * G * J])
        size = sb("size", [T, STEPS * G * J])
        ez = sb("ez", [T, STEPS * G * J])
        y = sb("y", [T, STEPS * G * J])

        ps_key, ps_s, ps_t = bank("ps_key"), bank("ps_s"), bank("ps_t")
        ps_val = ctx.enter_context(nc.psum_tensor("ps_val", [P, T, 512], F32))
        ps_y = [bank(f"ps_y{g}") for g in range(G)]
        ps_x = bank("ps_x")

        loaded = sem("loaded")
        small_loaded = sem("small_loaded")
        cat_loaded = sem("cat_loaded")
        zeroed = sem("zeroed")
        blank = sem("blank")
        const_made = sem("const_made")
        w_prod = sem("w_prod")
        w_kept = sem("w_kept")
        idx_step = sem("idx_step")

        W_LOADS, SMALL_LOADS = 6 + 2, 6
        with nc.Block() as block:
            @block.sync
            def _(sp):
                sp.dma_start(cat_sb[:], cat).then_inc(cat_loaded, 16)
                sp.dma_start(base_sb[:], cat_base).then_inc(cat_loaded, 16)
                sp.dma_start(wq_sb[:], wq.rearrange("l o i -> o l i")).then_inc(loaded, 16)
                sp.dma_start(wo_sb[:], wo_t.rearrange("l o i -> o l i")).then_inc(loaded, 16)
                for t in range(T):
                    sp.dma_start(wk_sb[:, :, t, :], wk.rearrange("l o i -> o l i")).then_inc(loaded, 16)
                    sp.dma_start(wv_sb[:, :, t, :], wv.rearrange("l o i -> o l i")).then_inc(loaded, 16)
                sp.wait_ge(zeroed, 1)
                for t in range(T):
                    sp.dma_start(res_w[E * t:E * (t + 1), :, t, :], wres_t.rearrange("l i o -> i l o")).then_inc(loaded, 16)

            @block.scalar
            def _(act):
                act.dma_start(num_sb[:], num).then_inc(small_loaded, 16)
                act.dma_start(num_w[:], w_num).then_inc(small_loaded, 16)
                act.dma_start(num_b[:], b_num).then_inc(small_loaded, 16)
                for t in range(T):
                    act.dma_start(fin_w[E * t:E * (t + 1), :], w_fin).then_inc(small_loaded, 16)
                act.dma_start(fin_b[:], b_fin).then_inc(small_loaded, 16)
                act.wait_ge(small_loaded, 16 * SMALL_LOADS)

            @block.gpsimd
            def _(pool):
                nc.gpsimd.memset(res_w[:], 0.0).then_inc(zeroed, 1)
                nc.gpsimd.memset(ident[:], 0.0)
                nc.gpsimd.memset(same[:], 1.0).then_inc(blank, 1)
                pool.wait_ge(blank, 1)
                nc.gpsimd.affine_select(out=ident[:], in_=ident[:], compare_op=ALU.not_equal, fill=1.0, base=0,
                                        pattern=[[-1, P]], channel_multiplier=1)
                nc.gpsimd.affine_select(out=same[:], in_=same[:], compare_op=ALU.is_ge, fill=0.0, base=0,
                                        pattern=[[-F, J]], channel_multiplier=1).then_inc(blank, 1)
                pool.wait_ge(blank, 2)
                nc.gpsimd.affine_select(out=same[:], in_=same[:], compare_op=ALU.is_ge, fill=0.0, base=F - 1,
                                        pattern=[[F, J]], channel_multiplier=-1).then_inc(const_made, 1)

            @block.vector
            def _(dve):
                for x in (*xt, *vals, probs, mix, partial, key_w, halves):
                    nc.vector.memset(x[:], 0.0 if x is not probs else 1.0)
                for x in (ps_s, ps_t, *ps_y):
                    nc.vector.memset(x[:], 0.0)
                nc.vector.memset(keys[:], 0.0).then_inc(w_kept, 1)
                dve.wait_ge(w_kept, 1)
                for t in range(T):
                    nc.vector.memset(halves[E * t:E * (t + 1), t:t + 1], 1.0)
                dve.wait_ge(cat_loaded, 32)
                nc.vector.tensor_copy(base_f[:], base_sb[:])
                nc.vector.tensor_copy(cat_f[:], cat_sb[:]).then_inc(idx_step, 1)
                dve.wait_ge(idx_step, 1)
                nc.vector.tensor_scalar(neg_f[:], cat_f[:], 0.0, float(VOCAB), ALU.is_lt, ALU.mult).then_inc(idx_step, 1)
                dve.wait_ge(idx_step, 2)
                nc.vector.tensor_tensor(neg_f[:], cat_f[:], neg_f[:], ALU.add).then_inc(idx_step, 1)
                dve.wait_ge(idx_step, 3)
                nc.vector.tensor_scalar(cat_f[:], neg_f[:], 0.0, float(VOCAB - 1), ALU.max, ALU.min).then_inc(idx_step, 1)
                dve.wait_ge(idx_step, 4)
                nc.vector.tensor_scalar(row_sb[:], cat_f[:], base_f[:, 0:1], None, ALU.add).then_inc(idx_step, 1)
                for n in range(L):
                    for h in range(H):
                        dve.wait_ge(w_prod, n * H + h + 1)
                        for t in range(T):
                            half = slice(E * t, E * (t + 1))
                            nc.vector.tensor_copy(key_w[half, n, h, t, :], ps_key[half, 0:E])
                        nc.vector.tensor_copy(val_w[:, n, h, :], ps_key[:, E:2 * E]).then_inc(w_kept, 1)

            @block.tensor
            def _(pe):
                pe.wait_ge(loaded, 16 * W_LOADS)
                for n in range(L):
                    for h in range(H):
                        pe.wait_ge(w_kept, 1 + n * H + h)
                        rows = slice(D * h, D * (h + 1))
                        nc.tensor.matmul(ps_key[:, 0:E], wk_sb[rows, n, :, :].rearrange("o t i -> o (t i)"), wq_sb[rows, n, :],
                                         start=True, stop=True)
                        nc.tensor.matmul(ps_key[:, E:2 * E], wv_sb[rows, n, :, :].rearrange("o t i -> o (t i)"), wo_sb[rows, n, :],
                                         start=True, stop=True).then_inc(w_prod, 1)

        rows_set = sem("rows_set")
        mul_done = sem("mul_done")
        gathered = [sem(f"gathered{n}") for n in range(NT)]
        num_ready = sem("num_ready")
        x_turned = sem("x_turned")
        x_ready = sem("x_ready")
        key_done = sem("key_done")
        key_ready = sem("key_ready")
        val_done = sem("val_done")
        val_ready = sem("val_ready")
        s_done = sem("s_done")
        top_ready = sem("top_ready")
        sub_ready = sem("sub_ready")
        exp_ready = sem("exp_ready")
        den_ready = sem("den_ready")
        inv_ready = sem("inv_ready")
        p_ready = sem("p_ready")
        t_done = sem("t_done")
        mix_act = sem("mix_act")
        mix_dve = sem("mix_dve")
        y_done = [sem(f"y_done{g}") for g in range(G)]
        y_used = [sem(f"y_used{g}") for g in range(G)]
        fin_done = sem("fin_done")
        primed = sem("primed")

        tab_rows = tables.rearrange("c v e -> (c v) e")
        probs_r = probs[:].rearrange("p g h j k -> p g j h k")
        mix_t = ps_t[0:TOK, :].rearrange("p (n q) -> p n q", q=E)

        with nc.Block() as block:
            @block.gpsimd
            def _(pool):
                def fetch(i):
                    nc.gpsimd.tensor_copy(rows_now[:], row_sb[:, bass.ds(i * NT, NT)]).then_inc(rows_set, 1)
                    nc.gpsimd.tensor_tensor(
                        tok_mul[:].rearrange("p g t e -> p (g t) e"),
                        num_w[:].unsqueeze(1).to_broadcast([NUM_ROWS, NT, E]),
                        num_sb[:, bass.ds(i * NT, NT)].unsqueeze(2).to_broadcast([NUM_ROWS, NT, E]),
                        ALU.mult).then_inc(mul_done, 1)
                    pool.wait_ge(rows_set, i + 1)
                    pool.wait_ge(mul_done, i + 1)
                    nc.gpsimd.tensor_tensor(
                        tok_num[:].rearrange("p g t e -> p (g t) e"), tok_mul[:].rearrange("p g t e -> p (g t) e"),
                        num_b[:].unsqueeze(1).to_broadcast([NUM_ROWS, NT, E]), ALU.add).then_inc(num_ready, 1)
                    for n in range(NT):
                        pool.indirect_dma_start(
                            out=tok_cat[:, n // T, n % T, :], out_offset=None, in_=tab_rows,
                            in_offset=bass.IndirectOffsetOnAxis(ap=rows_now[:, n:n + 1], axis=0),
                        ).then_inc(gathered[n], 16)

                fetch(0)
                with pool.Fori(0, STEPS) as i:
                    pool.wait_ge(x_turned, i + 1)
                    fetch(i + 1)
                for n in range(NT):
                    pool.wait_ge(gathered[n], 16 * (STEPS + 1))

            @block.tensor
            def _(pe):
                def turn(i):
                    for n in range(NT):
                        pe.wait_ge(gathered[n], 16 * (i + 1))
                    pe.wait_ge(num_ready, i + 1)
                    for g in range(G):
                        nc.tensor.transpose(ps_x[:, g * TOK:g * TOK + CAT_ROWS],
                                            tok_cat[:, g, :, :].rearrange("p t e -> p (t e)"), ident[0:CAT_ROWS, 0:CAT_ROWS])
                        last = nc.tensor.transpose(ps_x[:, g * TOK + CAT_ROWS:(g + 1) * TOK],
                                                   tok_num[:, g, :, :].rearrange("p t e -> p (t e)"), ident[0:NUM_ROWS, 0:NUM_ROWS])
                    last.then_inc(x_turned, 1)

                turn(0)
                with pe.Fori(0, STEPS) as i:
                    for w, (front, back) in enumerate(WINDOWS):
                        n = i * W + w
                        if front == 0:
                            pe.wait_ge(x_ready, i + 1)
                        for g in range(G):
                            pe.wait_ge(y_used[g], n + 1)
                            for h in range(H):
                                last = nc.tensor.matmul(ps_key[:, (h * G + g) * TOK:(h * G + g + 1) * TOK],
                                                        key_w[:, front, h, :, :].rearrange("p t e -> p (t e)"), xt[front][:, g, :],
                                                        start=True, stop=True, skip_group_check=True)
                        last.then_inc(key_done, 1)
                        pe.wait_ge(val_ready, n + 1)
                        for g in range(G):
                            for t in range(T):
                                half = slice(E * t, E * (t + 1))
                                c = g * H * E
                                last = nc.tensor.matmul(ps_val[0:TOK, t, c:c + H * E], xt[front][half, g, :],
                                                        val_w[half, front, :, :].rearrange("p h e -> p (h e)"),
                                                        start=True, stop=True, skip_group_check=True)
                        last.then_inc(val_done, 1)
                        pe.wait_ge(p_ready, n + 1)
                        for g in range(G):
                            for h in range(H):
                                c = (g * H + h) * P
                                last = nc.tensor.transpose(ps_t[0:TOK, c:c + P],
                                                           probs[:, g, h, :, :].rearrange("p j k -> p (j k)"), ident[:])
                        last.then_inc(t_done, 1)
                        def project(g):
                            nc.tensor.matmul(ps_y[g][:, 0:TOK], res_w[:, back, :, :].rearrange("p t e -> p (t e)"),
                                             xt[back][:, g, :], start=True, stop=False, skip_group_check=True)

                        pe.wait_ge(key_ready, n + 1)
                        pe.wait_ge(sub_ready, n + 1)
                        project(0)
                        for g in range(G):
                            for j in range(J):
                                for t in range(T):
                                    half = slice(E * t, E * (t + 1))
                                    c = (g * J + j) * H * F
                                    last = nc.tensor.matmul(ps_s[E * t:E * t + F, c:c + H * F],
                                                            xt[front][half, g, j * F:(j + 1) * F],
                                                            keys[half, g, j, :, :].rearrange("p h k -> p (h k)"),
                                                            start=True, stop=True, skip_group_check=True)
                        last.then_inc(s_done, 1)
                        for g in range(G):
                            if g == 0:
                                pe.wait_ge(mix_act, n + 1)
                                pe.wait_ge(mix_dve, n + 1)
                            else:
                                project(g)
                            for t in range(T):
                                for h in range(H):
                                    last = nc.tensor.matmul(ps_y[g][E * t:E * (t + 1), 0:TOK], vals[back][:, g, t, h, :],
                                                            mix[:, (g * H + h) * T + t, :, :].rearrange("p j q -> p (j q)"),
                                                            start=False, stop=(h == H - 1), skip_group_check=True)
                            last.then_inc(y_done[g], 1)
                        if w == W - 1:
                            turn(i + 1)

            @block.scalar
            def _(act):
                def take_x(i):
                    act.wait_ge(x_turned, i + 1)
                    nc.scalar.activation(xt[0][:].rearrange("p g (j f) -> p g j f", j=J),
                                         ps_x[:, 0:G * TOK].rearrange("p (g f j) -> p g j f", g=G, j=J),
                                         ACT.Copy).then_inc(x_ready, 1)

                def take_y(g, n, back):
                    act.wait_ge(y_done[g], n + 1)
                    nc.scalar.activation(xt[back + 1][:, g, :], ps_y[g][:, 0:TOK], ACT.Copy).then_inc(y_used[g], 1)

                for s in (val_ready, exp_ready):
                    act.sem_inc(s, 1)
                take_x(0)
                with act.Fori(0, STEPS) as i:
                    for w, (front, back) in enumerate(WINDOWS):
                        n = i * W + w
                        act.wait_ge(key_done, n + 1)
                        nc.scalar.activation(keys[:].rearrange("p g j h k -> p h (g j) k"),
                                             ps_key[:, 0:H * G * TOK].rearrange("p (h n k) -> p h n k", h=H, k=F),
                                             ACT.Copy).then_inc(key_ready, 1)
                        act.wait_ge(val_done, n + 1)
                        nc.scalar.activation(vals[front][:].rearrange("p g t h e -> p t g (h e)"),
                                             ps_val[0:TOK, :, 0:G * H * E].rearrange("p t (g x) -> p t g x", g=G),
                                             ACT.Copy).then_inc(val_ready, 1)
                        act.wait_ge(t_done, n + 1)
                        for j in range(J - 1):
                            last = nc.scalar.activation(mix[:, :, j, :], mix_t[:, :, 0:F], ACT.Copy,
                                                        scale=same[0:TOK, j:j + 1])
                        last.then_inc(mix_act, 1)
                        if back < L - 1:
                            take_y(0, n, back)
                        act.wait_ge(sub_ready, n + 2)
                        nc.scalar.activation(probs[:], probs[:], ACT.Exp, scale=SCALE).then_inc(exp_ready, 1)
                        if back < L - 1:
                            take_y(1, n, back)
                        if w == W - 1:
                            take_x(i + 1)

            @block.vector
            def _(dve):
                for s in (sub_ready, *y_used):
                    dve.sem_inc(s, 1)
                with dve.Fori(0, STEPS) as i:
                    for w, (front, back) in enumerate(WINDOWS):
                        n = i * W + w
                        dve.wait_ge(exp_ready, n + 1)
                        nc.vector.tensor_reduce(den[:], probs[:], AX, ALU.add).then_inc(den_ready, 1)
                        dve.wait_ge(den_ready, n + 1)
                        nc.vector.reciprocal(inv[:], den[:]).then_inc(inv_ready, 1)
                        dve.wait_ge(inv_ready, n + 1)
                        nc.vector.tensor_tensor(probs[:].rearrange("p g h j k -> p (g h j) k"),
                                                probs[:].rearrange("p g h j k -> p (g h j) k"),
                                                inv[:].rearrange("p g h j -> p (g h j)").unsqueeze(2).to_broadcast([P, G * H * J, F]),
                                                ALU.mult).then_inc(p_ready, 1)
                        dve.wait_ge(mix_act, n + 1)
                        nc.vector.tensor_scalar(mix[:, :, J - 1, :], mix_t[:, :, 0:F], same[0:TOK, J - 1:J], None,
                                                ALU.mult).then_inc(mix_dve, 1)
                        dve.wait_ge(s_done, n + 1)
                        scores = ps_s[:, 0:G * J * H * F].rearrange("p (r k) -> p r k", k=F)
                        nc.vector.tensor_reduce(top[:].rearrange("p g j h -> p (g j h)"), scores, AX, ALU.max).then_inc(top_ready, 1)
                        dve.wait_ge(top_ready, n + 1)
                        for g in range(G):
                            last = nc.vector.tensor_tensor(
                                probs_r[:, g], ps_s[:, g * J * H * F:(g + 1) * J * H * F].rearrange("p (j h k) -> p j h k", j=J, h=H),
                                top[:, g].unsqueeze(3).to_broadcast([P, J, H, F]), ALU.subtract)
                        last.then_inc(sub_ready, 1)
                        if back == L - 1:
                            for g in range(G):
                                dve.wait_ge(y_done[g], n + 1)
                                nc.vector.tensor_tensor(fin_x[:, g], ps_y[g][:, 0:TOK].rearrange("p (j f) -> p j f", j=J),
                                                        fin_w[:].unsqueeze(1).to_broadcast([P, J, F]), ALU.mult).then_inc(y_used[g], 1)
                            for g in range(G):
                                dve.wait_ge(y_used[g], n + 2)
                            nc.vector.tensor_reduce(partial[:, bass.ds(i, 1), :].rearrange("p s c -> p (s c)"),
                                                    fin_x[:].rearrange("p g j f -> p (g j) f"), AX, ALU.add).then_inc(fin_done, 1)

        z_done = sem("z_done")
        e_done = sem("e_done")
        y_step = sem("y_step")
        written = sem("written")
        NZ = STEPS * G * J
        cuts = [(a, min(512, NZ - a)) for a in range(0, NZ, 512)]
        banks = [ps_key, ps_t, ps_s]
        with nc.Block() as block:
            @block.tensor
            def _(pe):
                pe.wait_ge(fin_done, STEPS)
                flat = partial[:].rearrange("p s c -> p (s c)")
                for b, (a, m) in enumerate(cuts):
                    last = nc.tensor.matmul(banks[b][0:T, 0:m], halves[:], flat[:, a:a + m], start=True, stop=True)
                last.then_inc(z_done, 1)

            @block.vector
            def _(dve):
                dve.wait_ge(z_done, 1)
                for b, (a, m) in enumerate(cuts):
                    last = nc.vector.tensor_scalar(z[:, a:a + m], banks[b][0:T, 0:m], fin_b[:, 0:1], None, ALU.add)
                last.then_inc(y_step, 1)
                dve.wait_ge(y_step, 1)
                nc.vector.scalar_tensor_tensor(out=size[:], in0=z[:], scalar=-1.0, in1=z[:], op0=ALU.mult, op1=ALU.max).then_inc(y_step, 1)
                dve.wait_ge(e_done, 1)
                nc.vector.tensor_scalar(y[:], ez[:], 1.0, None, ALU.add).then_inc(y_step, 1)
                nc.vector.scalar_tensor_tensor(out=z[:], in0=z[:], scalar=0.0, in1=ez[:], op0=ALU.is_ge,
                                               op1=ALU.max).then_inc(y_step, 1)
                dve.wait_ge(y_step, 4)
                nc.vector.reciprocal(size[:], y[:]).then_inc(y_step, 1)
                dve.wait_ge(y_step, 5)
                nc.vector.tensor_tensor(y[:], z[:], size[:], ALU.mult).then_inc(y_step, 1)

            @block.scalar
            def _(act):
                act.wait_ge(y_step, 2)
                nc.scalar.activation(ez[:], size[:], ACT.Exp, scale=-1.0).then_inc(e_done, 1)

            @block.sync
            def _(sp):
                sp.wait_ge(y_step, 6)
                sp.dma_start(out, y[:]).then_inc(written, 16)
                sp.wait_ge(written, 16)


def kernel(**inputs):
    import numpy as np
    import concourse.bacc as bacc
    from concourse.bass_utils import run_bass_kernel_spmd as run

    a = {k.removeprefix("L0_rec_"): np.asarray(v) for k, v in inputs.items()}
    order = np.minimum(np.arange(COLS * J), B - 1)

    def by_triple(x):
        return np.ascontiguousarray(x[order].reshape(COLS, J, -1).transpose(2, 1, 0).reshape(-1, COLS))

    fin = a["W_final"].reshape(F, E)
    laid = {
        "num": by_triple(a["r_num_features"]),
        "cat": by_triple(a["r_cat_features"]),
        "cat_base": np.repeat(np.arange(NUM_CAT, dtype=np.int32) * VOCAB, J)[:, None],
        "w_num": np.repeat(a["W_num"], J, axis=0),
        "b_num": np.repeat(a["b_num"], J, axis=0),
        "tables": a["cat_tables"],
        "wq": a["W_Q"],
        "wk": a["W_K"],
        "wv": a["W_V"],
        "wo_t": a["W_O"].transpose(0, 2, 1),
        "wres_t": a["W_Res"].transpose(0, 2, 1),
        "w_fin": np.concatenate([fin[NUM_NUM:], fin[:NUM_NUM]]).T,
        "b_fin": np.repeat(a["b_final"][None], T, axis=0),
    }
    nc = bacc.Bacc("TRN2", target_bir_lowering=False, num_devices=1)
    arrays, args = {}, []
    for name, x in laid.items():
        x = np.ascontiguousarray(x)
        arrays[f"in_{name}"] = x
        args.append(nc.dram_tensor(f"in_{name}", x.shape, mybir.dt.from_np(x.dtype), kind="ExternalInput").ap())
    args.append(nc.dram_tensor("out_y", (T, STEPS * G * J), F32, kind="ExternalOutput").ap())
    recsys_attention(nc, *args)
    r = run(nc, [arrays], core_ids=[0])
    got = np.asarray(r.results[0]["out_y"]).reshape(T, STEPS, G, J)[:, 1:]
    return np.ascontiguousarray(got.transpose(1, 2, 0, 3).reshape(-1)[:B])
```

```python
from contextlib import ExitStack

import concourse.bass as bass
from concourse import mybir

F32 = mybir.dt.float32
I32 = mybir.dt.int32
U32 = mybir.dt.uint32
ALU = mybir.AluOpType
ACT = mybir.ActivationFunctionType
AX = mybir.AxisListType.X

B, NUM_NUM, NUM_CAT, VOCAB = 2048, 13, 26, 1250
E, L, H = 64, 3, 2
F = NUM_NUM + NUM_CAT
D = E // H

J = 3
T = 2
G = 2
TOK = J * F
CH = G * T * J
CHUNKS = -(-B // CH)
LAG = 3
STEPS = CHUNKS + LAG
NT = G * T
COLS = (STEPS + 2) * NT
CAT_ROWS = J * NUM_CAT
NUM_ROWS = J * NUM_NUM
P = 128
SCALE = float(D) ** -0.5



def recsys_attention(nc, num, cat, cat_base, w_num, b_num, tables, wq, wk, wv, wo_t, wres_t, wres_last, w_fin, b_fin, out):
    with ExitStack() as ctx:
        def sb(name, shape, dt=F32):
            return ctx.enter_context(nc.sbuf_tensor(name, shape, dt))

        def bank(name):
            return ctx.enter_context(nc.psum_tensor(name, [P, 512], F32))

        def sem(name):
            return ctx.enter_context(nc.semaphore(name))

        wq_sb = sb("wq_sb", [E, L, E])
        wk_sb = sb("wk_sb", [E, L, T, E])
        wv_sb = sb("wv_sb", [E, L, T, E])
        wo_sb = sb("wo_sb", [E, L, E])
        key_w = sb("key_w", [P, L, H, T, E])
        val_w = sb("val_w", [P, L, H, E])
        res_w = sb("res_w", [P, L, T, E])
        fin_w = sb("fin_w", [E, F])
        wres_sb = sb("wres_sb", [E, T, E])
        mixed_w = sb("mixed_w", [E, H, T, E])
        out_w = sb("out_w", [P, H, T, E])
        skip_w = sb("skip_w", [P, F])
        fin_b = sb("fin_b", [T, 1])
        num_w = sb("num_w", [NUM_ROWS, E])
        num_b = sb("num_b", [NUM_ROWS, E])
        ident = sb("ident", [P, P])
        same = sb("same", [P, J])
        halves = sb("halves", [P, T])
        cat_sb = sb("cat_sb", [CAT_ROWS, COLS], I32)
        base_sb = sb("base_sb", [CAT_ROWS, 1], I32)
        cat_f = sb("cat_f", [CAT_ROWS, COLS])
        neg_f = sb("neg_f", [CAT_ROWS, COLS])
        base_f = sb("base_f", [CAT_ROWS, 1])
        row_sb = sb("row_sb", [CAT_ROWS, COLS], U32)
        num_sb = sb("num_sb", [NUM_ROWS, COLS])
        rows_now = sb("rows_now", [CAT_ROWS, NT], U32)
        tok_cat = sb("tok_cat", [CAT_ROWS, G, T, E])
        tok_num = sb("tok_num", [NUM_ROWS, G, T, E])
        tok_mul = sb("tok_mul", [NUM_ROWS, G, T, E])
        xt = [sb(f"xt{n}", [P, G, TOK]) for n in range(L)]
        skip_in = sb("skip_in", [P, G, TOK])
        keys = sb("keys", [P, G, J, H, F])
        vals = [sb(f"vals{n}", [TOK, G, T, H, E]) for n in range(L - 1)]
        probs = [sb(f"probs{n}", [P, G, H, J, F]) for n in range(L)]
        worth = sb("worth", [P, H, G, J, F])
        gain = sb("gain", [P, H, G, J, F])
        skip = sb("skip", [P, G, J, F])
        num_h = sb("num_h", [P, H, G, J])
        part_h = sb("part_h", [P, H, G, J])
        top = sb("top", [P, G, J, H])
        den = sb("den", [P, G, H, J])
        inv = sb("inv", [P, G, H, J])
        mix = sb("mix", [TOK, G * H * T, J, F])
        partial = sb("partial", [P, STEPS, G * J])
        partial_skip = sb("partial_skip", [P, STEPS + 1, G * J])
        z = sb("z", [T, STEPS * G * J])
        size = sb("size", [T, STEPS * G * J])
        ez = sb("ez", [T, STEPS * G * J])
        y = sb("y", [T, STEPS * G * J])

        ps_key, ps_s, ps_t = bank("ps_key"), bank("ps_s"), bank("ps_t")
        ps_val = ctx.enter_context(nc.psum_tensor("ps_val", [P, T, 512], F32))
        ps_y = [bank(f"ps_y{g}") for g in range(G)]
        ps_x = bank("ps_x")

        loaded = sem("loaded")
        small_loaded = sem("small_loaded")
        cat_loaded = sem("cat_loaded")
        zeroed = sem("zeroed")
        blank = sem("blank")
        const_made = sem("const_made")
        w_prod = sem("w_prod")
        w_kept = sem("w_kept")
        head_made = sem("head_made")
        idx_step = sem("idx_step")

        W_LOADS, SMALL_LOADS = 6 + 2, 7
        with nc.Block() as block:
            @block.sync
            def _(sp):
                sp.dma_start(cat_sb[:], cat).then_inc(cat_loaded, 16)
                sp.dma_start(base_sb[:], cat_base).then_inc(cat_loaded, 16)
                sp.dma_start(wq_sb[:], wq.rearrange("l o i -> o l i")).then_inc(loaded, 16)
                sp.dma_start(wo_sb[:], wo_t.rearrange("l o i -> o l i")).then_inc(loaded, 16)
                for t in range(T):
                    sp.dma_start(wk_sb[:, :, t, :], wk.rearrange("l o i -> o l i")).then_inc(loaded, 16)
                    sp.dma_start(wv_sb[:, :, t, :], wv.rearrange("l o i -> o l i")).then_inc(loaded, 16)
                sp.wait_ge(zeroed, 1)
                for t in range(T):
                    sp.dma_start(res_w[E * t:E * (t + 1), :, t, :], wres_t.rearrange("l i o -> i l o")).then_inc(loaded, 16)

            @block.scalar
            def _(act):
                act.dma_start(num_sb[:], num).then_inc(small_loaded, 16)
                act.dma_start(num_w[:], w_num).then_inc(small_loaded, 16)
                act.dma_start(num_b[:], b_num).then_inc(small_loaded, 16)
                act.dma_start(fin_w[:], w_fin).then_inc(small_loaded, 16)
                for t in range(T):
                    act.dma_start(wres_sb[:, t, :], wres_last).then_inc(small_loaded, 16)
                act.dma_start(fin_b[:], b_fin).then_inc(small_loaded, 16)
                act.wait_ge(small_loaded, 16 * SMALL_LOADS)

            @block.gpsimd
            def _(pool):
                nc.gpsimd.memset(res_w[:], 0.0).then_inc(zeroed, 1)
                nc.gpsimd.memset(ident[:], 0.0)
                nc.gpsimd.memset(same[:], 1.0).then_inc(blank, 1)
                pool.wait_ge(blank, 1)
                nc.gpsimd.affine_select(out=ident[:], in_=ident[:], compare_op=ALU.not_equal, fill=1.0, base=0,
                                        pattern=[[-1, P]], channel_multiplier=1)
                nc.gpsimd.affine_select(out=same[:], in_=same[:], compare_op=ALU.is_ge, fill=0.0, base=0,
                                        pattern=[[-F, J]], channel_multiplier=1).then_inc(blank, 1)
                pool.wait_ge(blank, 2)
                nc.gpsimd.affine_select(out=same[:], in_=same[:], compare_op=ALU.is_ge, fill=0.0, base=F - 1,
                                        pattern=[[F, J]], channel_multiplier=-1).then_inc(const_made, 1)

            @block.vector
            def _(dve):
                for x in (*xt, skip_in, worth, partial_skip, *vals, mix, key_w, out_w, halves):
                    nc.vector.memset(x[:], 0.0)
                for x in probs:
                    nc.vector.memset(x[:], 1.0)
                for x in (ps_s, ps_t, *ps_y):
                    nc.vector.memset(x[:], 0.0)
                nc.vector.memset(keys[:], 0.0).then_inc(w_kept, 1)
                dve.wait_ge(w_kept, 1)
                for t in range(T):
                    nc.vector.memset(halves[E * t:E * (t + 1), t:t + 1], 1.0)
                dve.wait_ge(cat_loaded, 32)
                nc.vector.tensor_copy(base_f[:], base_sb[:])
                nc.vector.tensor_copy(cat_f[:], cat_sb[:]).then_inc(idx_step, 1)
                dve.wait_ge(idx_step, 1)
                nc.vector.tensor_scalar(neg_f[:], cat_f[:], 0.0, float(VOCAB), ALU.is_lt, ALU.mult).then_inc(idx_step, 1)
                dve.wait_ge(idx_step, 2)
                nc.vector.tensor_tensor(neg_f[:], cat_f[:], neg_f[:], ALU.add).then_inc(idx_step, 1)
                dve.wait_ge(idx_step, 3)
                nc.vector.tensor_scalar(cat_f[:], neg_f[:], 0.0, float(VOCAB - 1), ALU.max, ALU.min).then_inc(idx_step, 1)
                dve.wait_ge(idx_step, 4)
                nc.vector.tensor_scalar(row_sb[:], cat_f[:], base_f[:, 0:1], None, ALU.add).then_inc(idx_step, 1)
                for n in range(L):
                    for h in range(H):
                        dve.wait_ge(w_prod, n * H + h + 1)
                        for t in range(T):
                            half = slice(E * t, E * (t + 1))
                            nc.vector.tensor_copy(key_w[half, n, h, t, :], ps_key[half, 0:E])
                        nc.vector.tensor_copy(val_w[:, n, h, :], ps_key[:, E:2 * E]).then_inc(w_kept, 1)
                dve.wait_ge(w_prod, L * H + 1)
                for t in range(T):
                    last = nc.vector.tensor_copy(mixed_w[:, :, t, :], ps_key[0:E, 0:H * E].rearrange("p (h e) -> p h e", h=H))
                last.then_inc(w_kept, 1)
                dve.wait_ge(w_prod, L * H + 2)
                for h in range(H):
                    for t in range(T):
                        half = slice(E * t, E * (t + 1))
                        nc.vector.tensor_copy(out_w[half, h, t, 0:F], ps_key[half, h * F:(h + 1) * F])
                nc.vector.tensor_copy(skip_w[:], ps_key[:, H * F:(H + 1) * F]).then_inc(w_kept, 1)

            @block.tensor
            def _(pe):
                pe.wait_ge(loaded, 16 * W_LOADS)
                pe.wait_ge(small_loaded, 16 * SMALL_LOADS)
                for n in range(L):
                    for h in range(H):
                        pe.wait_ge(w_kept, 1 + n * H + h)
                        rows = slice(D * h, D * (h + 1))
                        nc.tensor.matmul(ps_key[:, 0:E], wk_sb[rows, n, :, :].rearrange("o t i -> o (t i)"), wq_sb[rows, n, :],
                                         start=True, stop=True)
                        nc.tensor.matmul(ps_key[:, E:2 * E], wv_sb[rows, n, :, :].rearrange("o t i -> o (t i)"), wo_sb[rows, n, :],
                                         start=True, stop=True).then_inc(w_prod, 1)
                for h in range(H):
                    pe.wait_ge(w_kept, 1 + L * H) if h == 0 else pe.wait_ge(head_made, h)
                    rows = slice(D * h, D * (h + 1))
                    last = nc.tensor.matmul(ps_key[0:E, h * E:(h + 1) * E], wo_sb[rows, L - 1, :], wv_sb[rows, L - 1, 0, :],
                                            start=True, stop=True, skip_group_check=True)
                    last.then_inc(head_made if h < H - 1 else w_prod, 1)
                pe.wait_ge(w_kept, 2 + L * H)
                for h in range(H):
                    nc.tensor.matmul(ps_key[:, h * F:(h + 1) * F], mixed_w[:, h, :, :].rearrange("e t i -> e (t i)"), fin_w[:],
                                     start=True, stop=True, skip_group_check=True)
                nc.tensor.matmul(ps_key[:, H * F:(H + 1) * F], wres_sb[:].rearrange("e t i -> e (t i)"), fin_w[:],
                                 start=True, stop=True, skip_group_check=True).then_inc(w_prod, 1)

        def each_layer(name):
            return [sem(f"{name}{n}") for n in range(L)]

        rows_set = sem("rows_set")
        mul_done = sem("mul_done")
        num_ready = sem("num_ready")
        gathered = sem("gathered")
        x_turned = sem("x_turned")
        x_ready = sem("x_ready")
        key_done = each_layer("key_done")
        key_ready = each_layer("key_ready")
        val_done = each_layer("val_done")
        val_ready = each_layer("val_ready")
        s_done = each_layer("s_done")
        top_ready = each_layer("top_ready")
        sub_ready = each_layer("sub_ready")
        exp_ready = each_layer("exp_ready")
        den_ready = each_layer("den_ready")
        inv_ready = each_layer("inv_ready")
        p_ready = each_layer("p_ready")
        t_done = each_layer("t_done")
        mix_ready = each_layer("mix_ready")
        y_done = [each_layer(f"y_done{g}_") for g in range(G)]
        y_ready = [each_layer(f"y_ready{g}_") for g in range(G)]
        gain_ready = sem("gain_ready")
        skip_ready = sem("skip_ready")
        skip_kept = sem("skip_kept")
        num_done = sem("num_done")
        part_done = sem("part_done")
        fin_done = sem("fin_done")

        tab_rows = tables.rearrange("c v e -> (c v) e")
        mix_t = ps_t[0:TOK, :].rearrange("p (n q) -> p n q", q=E)
        last_l = L - 1

        with nc.Block() as block:
            @block.gpsimd
            def _(pool):
                def fetch(i):
                    nc.gpsimd.tensor_copy(rows_now[:], row_sb[:, bass.ds(i * NT, NT)]).then_inc(rows_set, 1)
                    nc.gpsimd.tensor_tensor(
                        tok_mul[:].rearrange("p g t e -> p (g t) e"),
                        num_w[:].unsqueeze(1).to_broadcast([NUM_ROWS, NT, E]),
                        num_sb[:, bass.ds(i * NT, NT)].unsqueeze(2).to_broadcast([NUM_ROWS, NT, E]),
                        ALU.mult).then_inc(mul_done, 1)
                    pool.wait_ge(rows_set, i + 1)
                    pool.wait_ge(mul_done, i + 1)
                    nc.gpsimd.tensor_tensor(
                        tok_num[:].rearrange("p g t e -> p (g t) e"), tok_mul[:].rearrange("p g t e -> p (g t) e"),
                        num_b[:].unsqueeze(1).to_broadcast([NUM_ROWS, NT, E]), ALU.add).then_inc(num_ready, 1)
                    for n in range(NT):
                        pool.indirect_dma_start(
                            out=tok_cat[:, n // T, n % T, :], out_offset=None, in_=tab_rows,
                            in_offset=bass.IndirectOffsetOnAxis(ap=rows_now[:, n:n + 1], axis=0),
                        ).then_inc(gathered, 16)

                fetch(0)
                pool.wait_ge(x_turned, 1)
                fetch(1)
                with pool.Fori(0, STEPS) as i:
                    pool.wait_ge(val_ready[last_l], i + 1)
                    pool.wait_ge(exp_ready[last_l], i + 1)
                    nc.gpsimd.tensor_tensor(gain[:].rearrange("p h g j k -> p h g (j k)"),
                                            probs[last_l][:].rearrange("p g h j k -> p h g (j k)"),
                                            worth[:].rearrange("p h g j k -> p h g (j k)"), ALU.mult).then_inc(gain_ready, 1)
                    for g in range(G):
                        pool.wait_ge(y_ready[g][last_l - 1], i + 1)
                    pool.wait_ge(key_done[1], i + 1)
                    nc.gpsimd.tensor_tensor(skip[:].rearrange("p g j f -> p (g j) f"),
                                            xt[last_l][:].rearrange("p g (j f) -> p (g j) f", j=J),
                                            skip_w[:].unsqueeze(1).to_broadcast([P, G * J, F]), ALU.mult).then_inc(skip_ready, 1)
                    nc.gpsimd.tensor_copy(skip_in[:], xt[1][:]).then_inc(skip_kept, 1)
                    pool.wait_ge(x_turned, i + 2)
                    fetch(i + 2)
                pool.wait_ge(gathered, 16 * NT * (STEPS + 2))

            @block.tensor
            def _(pe):
                def turn(i):
                    pe.wait_ge(gathered, (i + 1) * (16 * NT))
                    pe.wait_ge(num_ready, i + 1)
                    for g in range(G):
                        nc.tensor.transpose(ps_x[:, g * TOK:g * TOK + CAT_ROWS],
                                            tok_cat[:, g, :, :].rearrange("p t e -> p (t e)"), ident[0:CAT_ROWS, 0:CAT_ROWS])
                        last = nc.tensor.transpose(ps_x[:, g * TOK + CAT_ROWS:(g + 1) * TOK],
                                                   tok_num[:, g, :, :].rearrange("p t e -> p (t e)"), ident[0:NUM_ROWS, 0:NUM_ROWS])
                    last.then_inc(x_turned, 1)

                def project_keys(n):
                    for g in range(G):
                        for h in range(H):
                            last = nc.tensor.matmul(ps_key[:, (h * G + g) * TOK:(h * G + g + 1) * TOK],
                                                    key_w[:, n, h, :, :].rearrange("p t e -> p (t e)"), xt[n][:, g, :],
                                                    start=True, stop=True, skip_group_check=True)
                    last.then_inc(key_done[n], 1)

                def project_values(n):
                    for g in range(G):
                        for t in range(T):
                            half = slice(E * t, E * (t + 1))
                            c = g * H * E
                            last = nc.tensor.matmul(ps_val[0:TOK, t, c:c + H * E], xt[n][half, g, :],
                                                    val_w[half, n, :, :].rearrange("p h e -> p (h e)"),
                                                    start=True, stop=True, skip_group_check=True)
                    last.then_inc(val_done[n], 1)

                def project_worth(i):
                    pe.wait_ge(val_ready[1], i + 1)
                    for h in range(H):
                        last = nc.tensor.matmul(ps_val[:, 0, h * G * TOK:(h + 1) * G * TOK],
                                                out_w[:, h, :, :].rearrange("p t q -> p (t q)"),
                                                xt[last_l][:].rearrange("p g x -> p (g x)"),
                                                start=True, stop=True, skip_group_check=True)
                    last.then_inc(val_done[last_l], 1)

                def turn_probs(n, i):
                    pe.wait_ge(p_ready[n], i + 1)
                    for g in range(G):
                        for h in range(H):
                            c = (g * H + h) * P
                            last = nc.tensor.transpose(ps_t[0:TOK, c:c + P],
                                                       probs[n][:, g, h, :, :].rearrange("p j k -> p (j k)"), ident[:])
                    last.then_inc(t_done[n], 1)

                def score(n):
                    for g in range(G):
                        for j in range(J):
                            for t in range(T):
                                half = slice(E * t, E * (t + 1))
                                c = (g * J + j) * H * F
                                last = nc.tensor.matmul(ps_s[E * t:E * t + F, c:c + H * F],
                                                        xt[n][half, g, j * F:(j + 1) * F],
                                                        keys[half, g, j, :, :].rearrange("p h k -> p (h k)"),
                                                        start=True, stop=True, skip_group_check=True)
                    last.then_inc(s_done[n], 1)

                def skip_into(n, g):
                    nc.tensor.matmul(ps_y[g][:, 0:TOK], res_w[:, n, :, :].rearrange("p t e -> p (t e)"),
                                     (skip_in if n else xt[0])[:, g, :], start=True, stop=False, skip_group_check=True)

                def mix_values(n, i):
                    pe.wait_ge(mix_ready[n], i + 1)
                    for g in range(G):
                        for h in range(H):
                            for t in range(T):
                                last = nc.tensor.matmul(ps_y[g][E * t:E * (t + 1), 0:TOK], vals[n][:, g, t, h, :],
                                                        mix[:, (g * H + h) * T + t, :, :].rearrange("p j q -> p (j q)"),
                                                        start=False, stop=(h == H - 1), skip_group_check=True)
                        last.then_inc(y_done[g][n], 1)

                turn(0)
                with pe.Fori(0, STEPS) as i:
                    pe.wait_ge(x_ready, i + 1)
                    project_keys(0)
                    project_values(0)
                    pe.wait_ge(y_ready[1][0], i + 1)
                    skip_into(1, 0)
                    pe.wait_ge(key_ready[0], i + 1)
                    skip_into(1, 1)
                    score(0)
                    mix_values(1, i)
                    project_keys(1)
                    pe.wait_ge(val_ready[0], i + 1)
                    project_values(1)
                    pe.wait_ge(key_ready[1], i + 1)
                    turn(i + 1)
                    score(1)
                    turn_probs(0, i)
                    project_keys(2)
                    project_worth(i)
                    skip_into(0, 0)
                    pe.wait_ge(sub_ready[1], i + 1)
                    pe.wait_ge(key_ready[2], i + 1)
                    skip_into(0, 1)
                    score(2)
                    pe.wait_ge(skip_kept, i + 1)
                    mix_values(0, i)
                    turn_probs(1, i)

            @block.scalar
            def _(act):
                def take_x(i):
                    act.wait_ge(x_turned, i + 1)
                    nc.scalar.activation(xt[0][:].rearrange("p g (j f) -> p g j f", j=J),
                                         ps_x[:, 0:G * TOK].rearrange("p (g f j) -> p g j f", g=G, j=J),
                                         ACT.Copy).then_inc(x_ready, 1)

                def take_keys(n, i):
                    act.wait_ge(key_done[n], i + 1)
                    nc.scalar.activation(keys[:].rearrange("p g j h k -> p h (g j) k"),
                                         ps_key[:, 0:H * G * TOK].rearrange("p (h n k) -> p h n k", h=H, k=F),
                                         ACT.Copy).then_inc(key_ready[n], 1)

                def take_values(n, i):
                    act.wait_ge(val_done[n], i + 1)
                    nc.scalar.activation(vals[n][:].rearrange("p g t h e -> p t g (h e)"),
                                         ps_val[0:TOK, :, 0:G * H * E].rearrange("p t (g x) -> p t g x", g=G),
                                         ACT.Copy).then_inc(val_ready[n], 1)

                def take_worth(i):
                    act.wait_ge(val_done[last_l], i + 1)
                    nc.scalar.activation(worth[:].rearrange("p h g j k -> p (h g j k)"), ps_val[:, 0, 0:H * G * TOK],
                                         ACT.Copy).then_inc(val_ready[last_l], 1)

                def spread(n, js, at):
                    act.wait_ge(t_done[n], at)
                    for j in js:
                        last = nc.scalar.activation(mix[:, :, j, :], mix_t[:, :, 0:F], ACT.Copy, scale=same[0:TOK, j:j + 1])
                    if j == J - 1:
                        last.then_inc(mix_ready[n], 1)

                def take_y(g, n, i):
                    act.wait_ge(y_done[g][n], i + 1)
                    nc.scalar.activation(xt[n + 1][:, g, :], ps_y[g][:, 0:TOK], ACT.Copy).then_inc(y_ready[g][n], 1)

                def exponentials(n, at):
                    act.wait_ge(sub_ready[n], at)
                    nc.scalar.activation(probs[n][:], probs[n][:], ACT.Exp, scale=SCALE).then_inc(exp_ready[n], 1)

                for s in (val_ready[2], t_done[1], *(y_ready[g][0] for g in range(G))):
                    act.sem_inc(s, 1)
                take_x(0)
                with act.Fori(0, STEPS) as i:
                    spread(1, (0,), i + 1)
                    exponentials(2, i + 1)
                    take_keys(0, i)
                    spread(1, (1, 2), i + 1)
                    take_values(0, i)
                    take_y(0, 1, i)
                    take_y(1, 1, i)
                    exponentials(0, i + 1)
                    take_keys(1, i)
                    take_values(1, i)
                    spread(0, (0, 1), i + 1)
                    take_keys(2, i)
                    exponentials(1, i + 1)
                    spread(0, (2,), i + 1)
                    take_worth(i)
                    act.wait_ge(s_done[2], i + 1)
                    take_x(i + 1)
                    take_y(0, 0, i)
                    take_y(1, 0, i)

            @block.vector
            def _(dve):
                def divide(n, i):
                    dve.wait_ge(exp_ready[n], i + 1)
                    nc.vector.tensor_reduce(den[:], probs[n][:], AX, ALU.add).then_inc(den_ready[n], 1)
                    dve.wait_ge(den_ready[n], i + 1)
                    nc.vector.reciprocal(inv[:], den[:]).then_inc(inv_ready[n], 1)
                    if n < last_l:
                        dve.wait_ge(inv_ready[n], i + 1)
                        nc.vector.tensor_tensor(probs[n][:].rearrange("p g h j k -> p (g h j) k"),
                                                probs[n][:].rearrange("p g h j k -> p (g h j) k"),
                                                inv[:].rearrange("p g h j -> p (g h j)").unsqueeze(2).to_broadcast([P, G * H * J, F]),
                                                ALU.mult).then_inc(p_ready[n], 1)

                def maxima(n, i):
                    dve.wait_ge(s_done[n], i + 1)
                    scores = ps_s[:, 0:G * J * H * F].rearrange("p (r k) -> p r k", k=F)
                    nc.vector.tensor_reduce(top[:].rearrange("p g j h -> p (g j h)"), scores, AX, ALU.max).then_inc(top_ready[n], 1)

                def subtract(n, i):
                    dve.wait_ge(top_ready[n], i + 1)
                    for g in range(G):
                        last = nc.vector.tensor_tensor(
                            probs[n][:, g].rearrange("p h j k -> p j h k"),
                            ps_s[:, g * J * H * F:(g + 1) * J * H * F].rearrange("p (j h k) -> p j h k", j=J, h=H),
                            top[:, g].unsqueeze(3).to_broadcast([P, J, H, F]), ALU.subtract)
                    last.then_inc(sub_ready[n], 1)

                def skip_logits(i):
                    dve.wait_ge(skip_ready, i + 1)
                    nc.vector.tensor_reduce(partial_skip[:, bass.ds(i + 1, 1), :].rearrange("p s c -> p (s c)"),
                                            skip[:].rearrange("p g j f -> p (g j) f"), AX, ALU.add)

                def sum_gains(i):
                    dve.wait_ge(gain_ready, i + 1)
                    nc.vector.tensor_reduce(num_h[:].rearrange("p h g j -> p (h g j)"),
                                            gain[:].rearrange("p h g j k -> p (h g j) k"), AX, ALU.add).then_inc(num_done, 1)

                def logits(i):
                    dve.wait_ge(inv_ready[last_l], i + 1)
                    dve.wait_ge(num_done, i + 1)
                    nc.vector.tensor_tensor(part_h[:], num_h[:], inv[:].rearrange("p g h j -> p h g j"), ALU.mult).then_inc(part_done, 1)
                    dve.wait_ge(part_done, i + 1)
                    nc.vector.tensor_tensor(partial[:, bass.ds(i, 1), :].rearrange("p s c -> p (s c)"),
                                            part_h[:, 0].rearrange("p g j -> p (g j)"), part_h[:, 1].rearrange("p g j -> p (g j)"),
                                            ALU.add).then_inc(fin_done, 1)

                dve.sem_inc(sub_ready[2], 1)
                with dve.Fori(0, STEPS) as i:
                    divide(2, i)
                    sum_gains(i)
                    maxima(0, i)
                    subtract(0, i)
                    logits(i)
                    divide(0, i)
                    maxima(1, i)
                    subtract(1, i)
                    skip_logits(i)
                    divide(1, i)
                    maxima(2, i)
                    subtract(2, i)

        z_done = sem("z_done")
        e_done = sem("e_done")
        y_step = sem("y_step")
        written = sem("written")
        NZ = STEPS * G * J
        cuts = [(a, min(512, NZ - a)) for a in range(0, NZ, 512)]
        banks = [ps_key, ps_t, ps_s]
        with nc.Block() as block:
            @block.tensor
            def _(pe):
                pe.wait_ge(fin_done, STEPS)
                parts = [x[:].rearrange("p s c -> p (s c)") for x in (partial, partial_skip)]
                for b, (a, m) in enumerate(cuts):
                    for x, part in enumerate(parts):
                        last = nc.tensor.matmul(banks[b][0:T, 0:m], halves[:], part[:, a:a + m], start=(x == 0), stop=(x == 1))
                last.then_inc(z_done, 1)

            @block.vector
            def _(dve):
                dve.wait_ge(z_done, 1)
                for b, (a, m) in enumerate(cuts):
                    last = nc.vector.tensor_scalar(z[:, a:a + m], banks[b][0:T, 0:m], fin_b[:, 0:1], None, ALU.add)
                last.then_inc(y_step, 1)
                dve.wait_ge(y_step, 1)
                nc.vector.scalar_tensor_tensor(out=size[:], in0=z[:], scalar=-1.0, in1=z[:], op0=ALU.mult, op1=ALU.max).then_inc(y_step, 1)
                dve.wait_ge(e_done, 1)
                nc.vector.tensor_scalar(y[:], ez[:], 1.0, None, ALU.add).then_inc(y_step, 1)
                nc.vector.scalar_tensor_tensor(out=z[:], in0=z[:], scalar=0.0, in1=ez[:], op0=ALU.is_ge,
                                               op1=ALU.max).then_inc(y_step, 1)
                dve.wait_ge(y_step, 4)
                nc.vector.reciprocal(size[:], y[:]).then_inc(y_step, 1)
                dve.wait_ge(y_step, 5)
                nc.vector.tensor_tensor(y[:], z[:], size[:], ALU.mult).then_inc(y_step, 1)

            @block.scalar
            def _(act):
                act.wait_ge(y_step, 2)
                nc.scalar.activation(ez[:], size[:], ACT.Exp, scale=-1.0).then_inc(e_done, 1)

            @block.sync
            def _(sp):
                sp.wait_ge(y_step, 6)
                sp.dma_start(out, y[:]).then_inc(written, 16)
                sp.wait_ge(written, 16)


def kernel(**inputs):
    import numpy as np
    import concourse.bacc as bacc
    from concourse.bass_utils import run_bass_kernel_spmd as run

    a = {k.removeprefix("L0_rec_"): np.asarray(v) for k, v in inputs.items()}
    order = np.minimum(np.arange(COLS * J), B - 1)

    def by_triple(x):
        return np.ascontiguousarray(x[order].reshape(COLS, J, -1).transpose(2, 1, 0).reshape(-1, COLS))

    fin = a["W_final"].reshape(F, E)
    laid = {
        "num": by_triple(a["r_num_features"]),
        "cat": by_triple(a["r_cat_features"]),
        "cat_base": np.repeat(np.arange(NUM_CAT, dtype=np.int32) * VOCAB, J)[:, None],
        "w_num": np.repeat(a["W_num"], J, axis=0),
        "b_num": np.repeat(a["b_num"], J, axis=0),
        "tables": a["cat_tables"],
        "wq": a["W_Q"],
        "wk": a["W_K"],
        "wv": a["W_V"],
        "wo_t": a["W_O"].transpose(0, 2, 1),
        "wres_t": a["W_Res"].transpose(0, 2, 1),
        "wres_last": a["W_Res"][L - 1],
        "w_fin": np.concatenate([fin[NUM_NUM:], fin[:NUM_NUM]]).T,
        "b_fin": np.repeat(a["b_final"][None], T, axis=0),
    }
    nc = bacc.Bacc("TRN2", target_bir_lowering=False, num_devices=1)
    arrays, args = {}, []
    for name, x in laid.items():
        x = np.ascontiguousarray(x)
        arrays[f"in_{name}"] = x
        args.append(nc.dram_tensor(f"in_{name}", x.shape, mybir.dt.from_np(x.dtype), kind="ExternalInput").ap())
    args.append(nc.dram_tensor("out_y", (T, STEPS * G * J), F32, kind="ExternalOutput").ap())
    recsys_attention(nc, *args)
    r = run(nc, [arrays], core_ids=[0])
    got = np.asarray(r.results[0]["out_y"]).reshape(T, STEPS, G, J)[:, LAG:]
    return np.ascontiguousarray(got.transpose(1, 2, 0, 3).reshape(-1)[:B])
```

```python
from contextlib import ExitStack

import concourse.bass as bass
from concourse import mybir

F32 = mybir.dt.float32
F32R = mybir.dt.float32r
I32 = mybir.dt.int32
U32 = mybir.dt.uint32
ALU = mybir.AluOpType
ACT = mybir.ActivationFunctionType
AX = mybir.AxisListType.X

B, NUM_NUM, NUM_CAT, VOCAB = 2048, 13, 26, 1250
E, L, H = 64, 3, 2
F = NUM_NUM + NUM_CAT
D = E // H

J = 3
T = 2
G = 2
TOK = J * F
CH = G * T * J
CHUNKS = -(-B // CH)
LAG = 3
STEPS = CHUNKS + LAG
NT = G * T
COLS = STEPS * NT
CAT_ROWS = J * NUM_CAT
NUM_ROWS = J * NUM_NUM
P = 128
SCALE = float(D) ** -0.5
R = G * J
ROWS = E + F



def recsys_attention(nc, num, cat, cat_base, w_num, b_num, tables, wq, wk, wv, wo_t, wres_t, wres_last, w_fin, b_fin, out):
    with ExitStack() as ctx:
        def sb(name, shape, dt=F32):
            return ctx.enter_context(nc.sbuf_tensor(name, shape, dt))

        def bank(name):
            return ctx.enter_context(nc.psum_tensor(name, [P, 512], F32))

        def sem(name):
            return ctx.enter_context(nc.semaphore(name))

        wq_sb = sb("wq_sb", [E, L, E])
        wk_sb = sb("wk_sb", [E, L, T, E])
        wv_sb = sb("wv_sb", [E, L, T, E])
        wo_sb = sb("wo_sb", [E, L, E])
        key_w = sb("key_w", [P, L, H, T, E])
        val_w = sb("val_w", [P, L - 1, T, H, E])
        res_w = sb("res_w", [P, L - 1, T, E])
        fin_w = sb("fin_w", [E, F])
        wres_sb = sb("wres_sb", [E, T, E])
        mixed_w = sb("mixed_w", [E, H, T, E])
        out_w = sb("out_w", [P, H, T, E])
        skip_w = sb("skip_w", [P, F])
        key_parts = [sb(f"key_{part}", [P, L, H, T, E], F32R) for part in ("hi", "lo")]
        val_parts = [sb(f"val_{part}", [P, L - 1, T, H, E], F32R) for part in ("hi", "lo")]
        res_parts = [sb(f"res_{part}", [P, L - 1, T, E], F32R) for part in ("hi", "lo")]
        out_parts = [sb(f"out_{part}", [P, H, T, E], F32R) for part in ("hi", "lo")]
        fin_b = sb("fin_b", [R * T, 1])
        num_w = sb("num_w", [NUM_ROWS, E])
        num_b = sb("num_b", [NUM_ROWS, E])
        ident = sb("ident", [P, P])
        same = sb("same", [P, J])
        sum_w = sb("sum_w", [P, R, R * T])
        cat_sb = sb("cat_sb", [CAT_ROWS, COLS], I32)
        base_sb = sb("base_sb", [CAT_ROWS, 1], I32)
        cat_f = sb("cat_f", [CAT_ROWS, COLS])
        neg_f = sb("neg_f", [CAT_ROWS, COLS])
        base_f = sb("base_f", [CAT_ROWS, 1])
        row_sb = sb("row_sb", [CAT_ROWS, COLS], U32)
        num_sb = sb("num_sb", [NUM_ROWS, COLS])
        rows_now = sb("rows_now", [CAT_ROWS, NT], U32)
        tok_cat = sb("tok_cat", [CAT_ROWS, G, T, E])
        tok_num = sb("tok_num", [NUM_ROWS, G, T, E])
        tok_mul = sb("tok_mul", [NUM_ROWS, G, T, E])
        xt = [sb(f"xt{n}", [P, G, TOK]) for n in range(L)]
        x_hi = [sb(f"x_hi{n}", [P, G, TOK], F32R) for n in range(L)]
        x_lo = [sb(f"x_lo{n}", [P, G, TOK], F32R) for n in range(L)]
        keys = [sb(f"keys{n}", [P, G, J, H, F]) for n in range(L)]
        vals = [sb(f"vals{n}", [TOK, G, T, H, E]) for n in range(L - 1)]
        probs = [sb(f"probs{n}", [P, G, H, J, F]) for n in range(L)]
        worth = sb("worth", [P, H, G, J, F])
        gain = sb("gain", [P, H, G, J, F])
        skip = sb("skip", [P, G, J, F])
        num_h = sb("num_h", [P, H, G, J])
        part_h = sb("part_h", [P, H, G, J])
        top = [sb(f"top{n}", [P, G, J, H]) for n in range(L)]
        den = [sb(f"den{n}", [P, G, H, J]) for n in range(L)]
        inv = [sb(f"inv{n}", [P, G, H, J]) for n in range(L)]
        mix = [sb(f"mix{n}", [TOK, G * H * T, J, F]) for n in range(L - 1)]
        partial = sb("partial", [P, STEPS, G * J])
        partial_skip = sb("partial_skip", [P, STEPS, G * J])
        z = sb("z", [R * T, STEPS])
        size = sb("size", [R * T, STEPS])
        ez = sb("ez", [R * T, STEPS])
        y = sb("y", [R * T, STEPS])

        ps_key, ps_s, ps_t = bank("ps_key"), bank("ps_s"), bank("ps_t")
        ps_val, ps_worth = bank("ps_val"), bank("ps_worth")
        ps_y = [bank(f"ps_y{n}") for n in range(L - 1)]
        ps_x = bank("ps_x")

        w_loaded = sem("w_loaded")
        res_loaded = sem("res_loaded")
        num_loaded = sem("num_loaded")
        fin_loaded = sem("fin_loaded")
        cat_loaded = sem("cat_loaded")
        zeroed = sem("zeroed")
        blank = sem("blank")
        w_blank = sem("w_blank")
        w_prod = sem("w_prod")
        mixed_kept = sem("mixed_kept")
        key_kept = sem("key_kept")
        out_kept = sem("out_kept")
        hi_made = sem("hi_made")
        idx_step = sem("idx_step")
        rows_set = sem("rows_set")
        mul_done = sem("mul_done")
        num_ready = sem("num_ready")
        gathered = sem("gathered")
        tab_rows = tables.rearrange("c v e -> (c v) e")

        def set_rows(i):
            nc.gpsimd.tensor_copy(rows_now[:], row_sb[:, bass.ds(i * NT, NT)]).then_inc(rows_set, 1)

        def multiply_numbers(i):
            nc.gpsimd.tensor_tensor(
                tok_mul[:].rearrange("p g t e -> p (g t) e"),
                num_w[:].unsqueeze(1).to_broadcast([NUM_ROWS, NT, E]),
                num_sb[:, bass.ds(i * NT, NT)].unsqueeze(2).to_broadcast([NUM_ROWS, NT, E]),
                ALU.mult).then_inc(mul_done, 1)

        def add_bias():
            nc.gpsimd.tensor_tensor(
                tok_num[:].rearrange("p g t e -> p (g t) e"), tok_mul[:].rearrange("p g t e -> p (g t) e"),
                num_b[:].unsqueeze(1).to_broadcast([NUM_ROWS, NT, E]), ALU.add).then_inc(num_ready, 1)

        def gather(pool, ns):
            for n in ns:
                pool.indirect_dma_start(
                    out=tok_cat[:, n // T, n % T, :], out_offset=None, in_=tab_rows,
                    in_offset=bass.IndirectOffsetOnAxis(ap=rows_now[:, n:n + 1], axis=0),
                ).then_inc(gathered, 16)

        with nc.Block() as block:
            @block.sync
            def _(sp):
                sp.dma_start(cat_sb[:], cat).then_inc(cat_loaded, 16)
                sp.dma_start(base_sb[:], cat_base).then_inc(cat_loaded, 16)
                for t in range(T):
                    sp.dma_start(wv_sb[:, :, t, :], wv.rearrange("l o i -> o l i")).then_inc(w_loaded, 16)
                    sp.dma_start(wk_sb[:, :, t, :], wk.rearrange("l o i -> o l i")).then_inc(w_loaded, 16)
                sp.wait_ge(zeroed, 1)
                for t in range(T):
                    sp.dma_start(res_w[E * t:E * (t + 1), :, t, :], wres_t.rearrange("l i o -> i l o")).then_inc(res_loaded, 16)

            @block.scalar
            def _(act):
                act.dma_start(wo_sb[:], wo_t.rearrange("l o i -> o l i")).then_inc(w_loaded, 16)
                act.dma_start(wq_sb[:], wq.rearrange("l o i -> o l i")).then_inc(w_loaded, 16)
                act.dma_start(num_sb[:], num).then_inc(num_loaded, 16)
                act.dma_start(num_w[:], w_num).then_inc(num_loaded, 16)
                act.dma_start(num_b[:], b_num).then_inc(num_loaded, 16)
                act.dma_start(fin_w[:], w_fin).then_inc(fin_loaded, 16)
                for t in range(T):
                    act.dma_start(wres_sb[:, t, :], wres_last).then_inc(fin_loaded, 16)
                act.dma_start(fin_b[:], b_fin).then_inc(fin_loaded, 16)
                act.wait_ge(w_blank, 1)
                for x in (*x_hi[1:], *x_lo[1:]):
                    nc.scalar.activation(x[:], xt[2][:], ACT.Copy)
                act.wait_ge(res_loaded, 16 * T)
                nc.scalar.activation(res_parts[0][:], res_w[:], ACT.Copy).then_inc(hi_made, 1)
                act.wait_ge(key_kept, 1)
                nc.scalar.activation(key_parts[0][:], key_w[:], ACT.Copy)
                nc.scalar.activation(val_parts[0][:], val_w[:], ACT.Copy).then_inc(hi_made, 1)
                act.wait_ge(out_kept, 1)
                nc.scalar.activation(out_parts[0][:], out_w[:], ACT.Copy).then_inc(hi_made, 1)

            @block.gpsimd
            def _(pool):
                nc.gpsimd.memset(res_w[:], 0.0).then_inc(zeroed, 1)
                nc.gpsimd.memset(ident[:], 0.0)
                nc.gpsimd.memset(same[:], 1.0).then_inc(blank, 1)
                pool.wait_ge(blank, 1)
                nc.gpsimd.affine_select(out=ident[:], in_=ident[:], compare_op=ALU.not_equal, fill=1.0, base=0,
                                        pattern=[[-1, P]], channel_multiplier=1)
                nc.gpsimd.affine_select(out=same[:], in_=same[:], compare_op=ALU.is_ge, fill=0.0, base=0,
                                        pattern=[[-F, J]], channel_multiplier=1).then_inc(blank, 1)
                pool.wait_ge(blank, 2)
                nc.gpsimd.affine_select(out=same[:], in_=same[:], compare_op=ALU.is_ge, fill=0.0, base=F - 1,
                                        pattern=[[F, J]], channel_multiplier=-1)
                nc.gpsimd.memset(vals[0][:], 0.0)
                nc.gpsimd.memset(mix[0][:], 0.0)
                pool.wait_ge(num_loaded, 16 * 3)
                pool.wait_ge(idx_step, 5)
                set_rows(0)
                multiply_numbers(0)
                pool.wait_ge(rows_set, 1)
                pool.wait_ge(mul_done, 1)
                add_bias()
                gather(pool, range(NT))

            @block.vector
            def _(dve):
                for x in (key_w, val_w, out_w, sum_w):
                    nc.vector.memset(x[:], 0.0)
                nc.vector.memset(xt[2][:], 0.0).then_inc(w_blank, 1)
                dve.wait_ge(cat_loaded, 32)
                nc.vector.tensor_copy(base_f[:], base_sb[:])
                nc.vector.tensor_copy(cat_f[:], cat_sb[:]).then_inc(idx_step, 1)
                dve.wait_ge(idx_step, 1)
                nc.vector.tensor_scalar(neg_f[:], cat_f[:], 0.0, float(VOCAB), ALU.is_lt, ALU.mult).then_inc(idx_step, 1)
                dve.wait_ge(idx_step, 2)
                nc.vector.tensor_tensor(neg_f[:], cat_f[:], neg_f[:], ALU.add).then_inc(idx_step, 1)
                dve.wait_ge(idx_step, 3)
                nc.vector.tensor_scalar(cat_f[:], neg_f[:], 0.0, float(VOCAB - 1), ALU.max, ALU.min).then_inc(idx_step, 1)
                dve.wait_ge(idx_step, 4)
                nc.vector.tensor_scalar(row_sb[:], cat_f[:], base_f[:, 0:1], None, ALU.add).then_inc(idx_step, 1)
                nc.vector.memset(keys[2][:], 0.0)
                nc.vector.memset(probs[1][:], 1.0)
                for x in (ps_s, *ps_y):
                    nc.vector.memset(x[:], 0.0)
                for r in range(R):
                    for t in range(T):
                        nc.vector.memset(sum_w[E * t:E * (t + 1), r, r * T + t:r * T + t + 1], 1.0)
                for h, ps in enumerate((ps_val, ps_worth)):
                    dve.wait_ge(w_prod, h + 1)
                    last = nc.vector.tensor_copy(mixed_w[:, h, :, :], ps[0:E, 0:E].unsqueeze(1).to_broadcast([E, T, E]))
                last.then_inc(mixed_kept, 1)
                for h, ps in enumerate((ps_key, ps_t)):
                    dve.wait_ge(w_prod, H + h + 1)
                    both = ps[:, 0:L * 2 * E].rearrange("p (n x) -> p n x", n=L)
                    for t in range(T):
                        half = slice(E * t, E * (t + 1))
                        nc.vector.tensor_copy(key_w[half, :, h, t, :], both[half, :, 0:E])
                        last = nc.vector.tensor_copy(val_w[half, :, t, h, :], both[half, 0:L - 1, E:2 * E])
                last.then_inc(key_kept, 1)
                dve.wait_ge(w_prod, 2 * H + 1)
                for t in range(T):
                    half = slice(E * t, E * (t + 1))
                    last = nc.vector.tensor_copy(out_w[half, :, t, 0:F], ps_x[half, 0:H * F].rearrange("p (h f) -> p h f", h=H))
                last.then_inc(out_kept, 1)
                nc.vector.tensor_copy(skip_w[:], ps_x[:, H * F:(H + 1) * F])
                for k, names in enumerate((((res_w, res_parts),), ((key_w, key_parts), (val_w, val_parts)), ((out_w, out_parts),))):
                    dve.wait_ge(hi_made, k + 1)
                    for whole, (hi, lo) in names:
                        nc.vector.tensor_tensor(lo[:], whole[:], hi[:], ALU.subtract)

            @block.tensor
            def _(pe):
                pe.wait_ge(w_loaded, 16 * (2 + 2 * T))
                for h, ps in enumerate((ps_val, ps_worth)):
                    rows = slice(D * h, D * (h + 1))
                    nc.tensor.matmul(ps[0:E, 0:E], wo_sb[rows, L - 1, :], wv_sb[rows, L - 1, 0, :],
                                     start=True, stop=True, skip_group_check=True).then_inc(w_prod, 1)
                for h, ps in enumerate((ps_key, ps_t)):
                    rows = slice(D * h, D * (h + 1))
                    for n in range(L):
                        c = n * 2 * E
                        last = nc.tensor.matmul(ps[:, c:c + E], wk_sb[rows, n, :, :].rearrange("o t i -> o (t i)"),
                                                wq_sb[rows, n, :], start=True, stop=True, skip_group_check=True)
                        if n < L - 1:
                            nc.tensor.matmul(ps[:, c + E:c + 2 * E], wv_sb[rows, n, :, :].rearrange("o t i -> o (t i)"),
                                             wo_sb[rows, n, :], start=True, stop=True, skip_group_check=True)
                    last.then_inc(w_prod, 1)
                pe.wait_ge(fin_loaded, 16 * (2 + T))
                pe.wait_ge(mixed_kept, 1)
                for h in range(H):
                    nc.tensor.matmul(ps_x[:, h * F:(h + 1) * F], mixed_w[:, h, :, :].rearrange("e t i -> e (t i)"), fin_w[:],
                                     start=True, stop=True, skip_group_check=True)
                nc.tensor.matmul(ps_x[:, H * F:(H + 1) * F], wres_sb[:].rearrange("e t i -> e (t i)"), fin_w[:],
                                 start=True, stop=True, skip_group_check=True).then_inc(w_prod, 1)

        def each_layer(name, layers=L):
            return [sem(f"{name}{n}") for n in range(layers)]

        x_turned = sem("x_turned")
        hi_ready = each_layer("hi_ready")
        lo_ready = each_layer("lo_ready")
        key_done = each_layer("key_done")
        key_ready = each_layer("key_ready")
        val_done = each_layer("val_done")
        val_ready = each_layer("val_ready")
        s_done = each_layer("s_done")
        top_ready = each_layer("top_ready")
        sub_ready = each_layer("sub_ready")
        exp_ready = each_layer("exp_ready")
        den_ready = each_layer("den_ready")
        inv_ready = each_layer("inv_ready")
        p_ready = each_layer("p_ready", L - 1)
        t_done = each_layer("t_done", L - 1)
        mix_ready = each_layer("mix_ready", L - 1)
        y_done = each_layer("y_done", L - 1)
        gain_ready = sem("gain_ready")
        skip_ready = sem("skip_ready")
        num_done = sem("num_done")
        part_done = sem("part_done")
        fin_done = sem("fin_done")

        z_done = sem("z_done")
        e_done = sem("e_done")
        y_step = sem("y_step")
        written = sem("written")

        mix_t = ps_t[0:TOK, :].rearrange("p (n q) -> p n q", q=E)
        last_l = L - 1

        with nc.Block() as block:
            @block.gpsimd
            def _(pool):
                def multiply_skip():
                    nc.gpsimd.tensor_tensor(skip[:].rearrange("p g j f -> p (g j) f"),
                                            xt[last_l][:].rearrange("p g (j f) -> p (g j) f", j=J),
                                            skip_w[:].unsqueeze(1).to_broadcast([P, G * J, F]), ALU.mult).then_inc(skip_ready, 1)

                def multiply_worth(i):
                    pool.wait_ge(val_ready[last_l], i + 1)
                    nc.gpsimd.tensor_tensor(gain[:].rearrange("p h g j k -> p h g (j k)"),
                                            probs[last_l][:].rearrange("p g h j k -> p h g (j k)"),
                                            worth[:].rearrange("p h g j k -> p h g (j k)"), ALU.mult).then_inc(gain_ready, 1)

                with pool.Fori(0, STEPS - 1) as i:
                    pool.wait_ge(x_turned, i + 1)
                    set_rows(i + 1)
                    pool.wait_ge(rows_set, i + 2)
                    pool.wait_ge(hi_ready[0], i + 1)
                    nc.gpsimd.tensor_tensor(x_lo[0][:], xt[0][:], x_hi[0][:], ALU.subtract).then_inc(lo_ready[0], 1)
                    gather(pool, range(NT // 2))
                    multiply_numbers(i + 1)
                    pool.wait_ge(mul_done, i + 2)
                    add_bias()
                    multiply_skip()
                    gather(pool, range(NT // 2, NT))
                    multiply_worth(i)
                multiply_skip()
                multiply_worth(STEPS - 1)
                pool.wait_ge(gathered, 16 * NT * STEPS)

            @block.tensor
            def _(pe):
                def turn(i):
                    pe.wait_ge(gathered, (i + 1) * (16 * NT))
                    pe.wait_ge(num_ready, i + 1)
                    for g in range(G):
                        nc.tensor.transpose(ps_x[:, g * TOK:g * TOK + CAT_ROWS],
                                            tok_cat[:, g, :, :].rearrange("p t e -> p (t e)"), ident[0:CAT_ROWS, 0:CAT_ROWS])
                        last = nc.tensor.transpose(ps_x[:, g * TOK + CAT_ROWS:(g + 1) * TOK],
                                                   tok_num[:, g, :, :].rearrange("p t e -> p (t e)"), ident[0:NUM_ROWS, 0:NUM_ROWS])
                    last.then_inc(x_turned, 1)

                def by_parts(out, w_parts, x_parts, passes=range(3), stop=True):
                    for k in passes:
                        w, x = ((0, 0), (0, 1), (1, 0))[k]
                        last = nc.tensor.matmul(out, w_parts[w], x_parts[x], start=(k == 0), stop=(stop and k == 2), skip_group_check=True)
                    return last

                def flat(parts, *at):
                    names = "abcd"[:len(parts[0].shape) - 1 - len(at)]
                    return [x[(slice(None), *at)].rearrange(f"p {' '.join(names)} -> p ({' '.join(names)})") for x in parts]

                def project_keys(n, h, passes=range(3)):
                    last = by_parts(ps_key[:, h * G * TOK:(h + 1) * G * TOK], flat(key_parts, n, h), flat((x_hi[n], x_lo[n])), passes)
                    if h == H - 1 and passes[-1] == 2:
                        last.then_inc(key_done[n], 1)

                def project_values(n):
                    for g in range(G):
                        last = by_parts(ps_val[0:TOK, g * T * H * E:(g + 1) * T * H * E], (x_hi[n][:, g, :], x_lo[n][:, g, :]),
                                        flat(val_parts, n))
                    last.then_inc(val_done[n], 1)

                def project_worth(h, passes=range(3)):
                    last = by_parts(ps_worth[:, h * G * TOK:(h + 1) * G * TOK], flat(out_parts, h),
                                    flat((x_hi[last_l], x_lo[last_l])), passes)
                    if h == H - 1 and passes[-1] == 2:
                        last.then_inc(val_done[last_l], 1)

                def turn_probs(n):
                    for g in range(G):
                        for h in range(H):
                            c = (g * H + h) * P
                            last = nc.tensor.transpose(ps_t[0:TOK, c:c + ROWS],
                                                       probs[n][0:ROWS, g, h, :, :].rearrange("p j k -> p (j k)"), ident[0:ROWS, 0:ROWS])
                    last.then_inc(t_done[n], 1)

                def score(n):
                    for g in range(G):
                        for j in range(J):
                            for t in range(T):
                                half = slice(E * t, E * (t + 1))
                                c = (g * J + j) * H * F
                                last = nc.tensor.matmul(ps_s[E * t:E * t + F, c:c + H * F],
                                                        xt[n][half, g, j * F:(j + 1) * F],
                                                        keys[n][half, g, j, :, :].rearrange("p h k -> p (h k)"),
                                                        start=True, stop=True, skip_group_check=True)
                    last.then_inc(s_done[n], 1)

                def skip_into(n, passes=range(3)):
                    by_parts(ps_y[n][:, 0:G * TOK], flat(res_parts, n), flat((x_hi[n], x_lo[n])), passes, stop=False)

                def mix_values(n):
                    for g in range(G):
                        for h in range(H):
                            for t in range(T):
                                last = nc.tensor.matmul(ps_y[n][E * t:E * (t + 1), g * TOK:(g + 1) * TOK], vals[n][:, g, t, h, :],
                                                        mix[n][:, (g * H + h) * T + t, :, :].rearrange("p j q -> p (j q)"),
                                                        start=False, stop=(h == H - 1), skip_group_check=True)
                    last.then_inc(y_done[n], 1)

                turn(0)
                with pe.Fori(0, STEPS - 1) as i:
                    pe.wait_ge(val_ready[0], i + 1)
                    project_values(1)
                    pe.wait_ge(key_ready[2], i + 1)
                    pe.wait_ge(lo_ready[0], i + 1)
                    project_keys(0, 0)
                    project_keys(0, 1, (0, 1))
                    pe.wait_ge(sub_ready[1], i + 1)
                    project_keys(0, 1, (2,))
                    score(2)
                    pe.wait_ge(mix_ready[0], i + 1)
                    mix_values(0)
                    pe.wait_ge(p_ready[1], i + 1)
                    turn_probs(1)
                    pe.wait_ge(key_ready[0], i + 1)
                    project_worth(0)
                    project_worth(1, (0, 1))
                    pe.wait_ge(sub_ready[2], i + 1)
                    project_worth(1, (2,))
                    score(0)
                    pe.wait_ge(mix_ready[1], i + 1)
                    mix_values(1)
                    pe.wait_ge(lo_ready[1], i + 1)
                    project_keys(1, 0)
                    project_keys(1, 1)
                    project_values(0)
                    pe.wait_ge(hi_ready[2], i + 1)
                    skip_into(1)
                    pe.wait_ge(sub_ready[0], i + 1)
                    skip_into(0, (0, 1))
                    pe.wait_ge(key_ready[1], i + 1)
                    skip_into(0, (2,))
                    score(1)
                    turn(i + 1)
                    pe.wait_ge(lo_ready[2], i + 1)
                    project_keys(2, 0)
                    project_keys(2, 1)
                    pe.wait_ge(p_ready[0], i + 1)
                    turn_probs(0)
                pe.wait_ge(key_ready[2], STEPS)
                project_worth(0)
                project_worth(1, (0, 1))
                pe.wait_ge(sub_ready[1], STEPS)
                project_worth(1, (2,))
                score(2)
                pe.wait_ge(fin_done, STEPS)
                for r in range(R):
                    for x, part in enumerate((partial, partial_skip)):
                        last = nc.tensor.matmul(ps_x[0:R * T, 0:STEPS], sum_w[:, r, :], part[:, :, r],
                                                start=(r == 0 and x == 0), stop=(r == R - 1 and x == 1))
                last.then_inc(z_done, 1)

            @block.scalar
            def _(act):
                def take_x(i):
                    act.wait_ge(x_turned, i + 1)
                    for x in (xt[0], x_hi[0]):
                        last = nc.scalar.activation(x[:].rearrange("p g (j f) -> p g j f", j=J),
                                                    ps_x[:, 0:G * TOK].rearrange("p (g f j) -> p g j f", g=G, j=J), ACT.Copy)
                    last.then_inc(hi_ready[0], 1)

                def take_keys(n):
                    nc.scalar.activation(keys[n][:].rearrange("p g j h k -> p h (g j) k"),
                                         ps_key[:, 0:H * G * TOK].rearrange("p (h n k) -> p h n k", h=H, k=F),
                                         ACT.Copy).then_inc(key_ready[n], 1)

                def take_values(n):
                    nc.scalar.activation(vals[n][:].rearrange("p g t h e -> p (g t h e)"), ps_val[0:TOK, :], ACT.Copy).then_inc(val_ready[n], 1)

                def take_worth():
                    nc.scalar.activation(worth[:].rearrange("p h g j k -> p (h g j k)"), ps_worth[:, 0:H * G * TOK],
                                         ACT.Copy).then_inc(val_ready[last_l], 1)

                def spread(n, js):
                    for j in js:
                        last = nc.scalar.activation(mix[n][:, :, j, :], mix_t[:, :, 0:F], ACT.Copy, scale=same[0:TOK, j:j + 1])
                    if j == J - 1:
                        last.then_inc(mix_ready[n], 1)

                def take_y(n, i):
                    act.wait_ge(y_done[n], i + 1)
                    nc.scalar.activation(xt[n + 1][:].rearrange("p g x -> p (g x)"), ps_y[n][:, 0:G * TOK], ACT.Copy)

                def take_high(n):
                    nc.scalar.activation(x_hi[n + 1][:].rearrange("p g x -> p (g x)"), ps_y[n][:, 0:G * TOK],
                                         ACT.Copy).then_inc(hi_ready[n + 1], 1)

                def exponentials(n):
                    nc.scalar.activation(probs[n][:], probs[n][:], ACT.Exp, scale=SCALE).then_inc(exp_ready[n], 1)

                for s in (mix_ready[0], val_ready[0], key_ready[2]):
                    act.sem_inc(s, 1)
                take_x(0)
                with act.Fori(0, STEPS - 1) as i:
                    act.wait_ge(val_done[1], i + 1)
                    take_values(1)
                    act.wait_ge(key_done[0], i + 1)
                    take_keys(0)
                    take_y(0, i)
                    act.wait_ge(t_done[1], i + 1)
                    spread(1, (0, 1, 2))
                    take_high(0)
                    act.wait_ge(sub_ready[2], i + 1)
                    exponentials(2)
                    act.wait_ge(skip_ready, i + 1)
                    take_y(1, i)
                    take_high(1)
                    act.wait_ge(key_done[1], i + 1)
                    take_keys(1)
                    act.wait_ge(sub_ready[0], i + 1)
                    exponentials(0)
                    take_worth()
                    act.wait_ge(val_done[0], i + 1)
                    take_values(0)
                    take_x(i + 1)
                    act.wait_ge(key_done[2], i + 1)
                    take_keys(2)
                    act.wait_ge(t_done[0], i + 1)
                    spread(0, (0,))
                    act.wait_ge(sub_ready[1], i + 2)
                    exponentials(1)
                    spread(0, (1, 2))
                act.wait_ge(sub_ready[2], STEPS)
                exponentials(2)
                act.wait_ge(val_done[last_l], STEPS)
                take_worth()
                act.wait_ge(y_step, 2)
                nc.scalar.activation(ez[:], size[:], ACT.Exp, scale=-1.0).then_inc(e_done, 1)

            @block.vector
            def _(dve):
                def sums(n, i):
                    dve.wait_ge(exp_ready[n], i + 1)
                    nc.vector.tensor_reduce(den[n][:], probs[n][:], AX, ALU.add).then_inc(den_ready[n], 1)

                def invert(n, i):
                    dve.wait_ge(den_ready[n], i + 1)
                    nc.vector.reciprocal(inv[n][:], den[n][:]).then_inc(inv_ready[n], 1)

                def probabilities(n, i):
                    dve.wait_ge(inv_ready[n], i + 1)
                    nc.vector.tensor_tensor(probs[n][:].rearrange("p g h j k -> p (g h j) k"),
                                            probs[n][:].rearrange("p g h j k -> p (g h j) k"),
                                            inv[n][:].rearrange("p g h j -> p (g h j)").unsqueeze(2).to_broadcast([P, G * H * J, F]),
                                            ALU.mult).then_inc(p_ready[n], 1)

                def maxima(n, i):
                    dve.wait_ge(s_done[n], i + 1)
                    for g in range(G):
                        nc.vector.tensor_reduce(top[n][:, g].rearrange("p j h -> p (j h)"),
                                                ps_s[:, g * J * H * F:(g + 1) * J * H * F].rearrange("p (r k) -> p r k", k=F),
                                                AX, ALU.max).then_inc(top_ready[n], 1)

                def subtract(n, i):
                    for g in range(G):
                        dve.wait_ge(top_ready[n], i * G + (g + 1))
                        last = nc.vector.tensor_tensor(
                            probs[n][:, g].rearrange("p h j k -> p j h k"),
                            ps_s[:, g * J * H * F:(g + 1) * J * H * F].rearrange("p (j h k) -> p j h k", j=J, h=H),
                            top[n][:, g].unsqueeze(3).to_broadcast([P, J, H, F]), ALU.subtract)
                    last.then_inc(sub_ready[n], 1)

                def low_part(n, i):
                    dve.wait_ge(hi_ready[n], i + 1)
                    nc.vector.tensor_tensor(x_lo[n][:], xt[n][:], x_hi[n][:], ALU.subtract).then_inc(lo_ready[n], 1)

                def skip_logits(i):
                    dve.wait_ge(skip_ready, i + 1)
                    nc.vector.tensor_reduce(partial_skip[:, bass.ds(i, 1), :].rearrange("p s c -> p (s c)"),
                                            skip[:].rearrange("p g j f -> p (g j) f"), AX, ALU.add)

                def head_logits(i):
                    dve.wait_ge(gain_ready, i + 1)
                    nc.vector.tensor_reduce(num_h[:].rearrange("p h g j -> p (h g j)"),
                                            gain[:].rearrange("p h g j k -> p (h g j) k"), AX, ALU.add).then_inc(num_done, 1)
                    dve.wait_ge(inv_ready[last_l], i + 1)
                    dve.wait_ge(num_done, i + 1)
                    nc.vector.tensor_tensor(part_h[:], num_h[:], inv[last_l][:].rearrange("p g h j -> p h g j"), ALU.mult).then_inc(part_done, 1)

                def add_heads(i):
                    dve.wait_ge(part_done, i + 1)
                    nc.vector.tensor_tensor(partial[:, bass.ds(i, 1), :].rearrange("p s c -> p (s c)"),
                                            part_h[:, 0].rearrange("p g j -> p (g j)"), part_h[:, 1].rearrange("p g j -> p (g j)"),
                                            ALU.add).then_inc(fin_done, 1)

                for s in (p_ready[1], sub_ready[1]):
                    dve.sem_inc(s, 1)
                with dve.Fori(0, STEPS - 1) as i:
                    maxima(2, i)
                    subtract(2, i)
                    skip_logits(i)
                    low_part(1, i)
                    maxima(0, i)
                    subtract(0, i)
                    sums(2, i)
                    low_part(2, i)
                    invert(2, i)
                    sums(0, i)
                    invert(0, i)
                    probabilities(0, i)
                    maxima(1, i)
                    subtract(1, i)
                    head_logits(i)
                    sums(1, i)
                    invert(1, i)
                    add_heads(i)
                    probabilities(1, i)
                maxima(2, STEPS - 1)
                subtract(2, STEPS - 1)
                skip_logits(STEPS - 1)
                sums(2, STEPS - 1)
                invert(2, STEPS - 1)
                head_logits(STEPS - 1)
                add_heads(STEPS - 1)
                dve.wait_ge(z_done, 1)
                nc.vector.tensor_scalar(z[:], ps_x[0:R * T, 0:STEPS], fin_b[:, 0:1], None, ALU.add).then_inc(y_step, 1)
                dve.wait_ge(y_step, 1)
                nc.vector.scalar_tensor_tensor(out=size[:], in0=z[:], scalar=-1.0, in1=z[:], op0=ALU.mult, op1=ALU.max).then_inc(y_step, 1)
                dve.wait_ge(e_done, 1)
                nc.vector.tensor_scalar(y[:], ez[:], 1.0, None, ALU.add).then_inc(y_step, 1)
                nc.vector.scalar_tensor_tensor(out=z[:], in0=z[:], scalar=0.0, in1=ez[:], op0=ALU.is_ge,
                                               op1=ALU.max).then_inc(y_step, 1)
                dve.wait_ge(y_step, 3)
                nc.vector.reciprocal(size[:], y[:]).then_inc(y_step, 1)
                dve.wait_ge(y_step, 5)
                nc.vector.tensor_tensor(y[:], z[:], size[:], ALU.mult).then_inc(y_step, 1)

            @block.sync
            def _(sp):
                sp.wait_ge(y_step, 6)
                sp.dma_start(out, y[:]).then_inc(written, 16)
                sp.wait_ge(written, 16)


def kernel(**inputs):
    import numpy as np
    import concourse.bacc as bacc
    from concourse.bass_utils import run_bass_kernel_spmd as run

    a = {k.removeprefix("L0_rec_"): np.asarray(v) for k, v in inputs.items()}
    order = np.minimum(np.arange(COLS * J), B - 1)

    def by_triple(x):
        return np.ascontiguousarray(x[order].reshape(COLS, J, -1).transpose(2, 1, 0).reshape(-1, COLS))

    fin = a["W_final"].reshape(F, E)
    laid = {
        "num": by_triple(a["r_num_features"]),
        "cat": by_triple(a["r_cat_features"]),
        "cat_base": np.repeat(np.arange(NUM_CAT, dtype=np.int32) * VOCAB, J)[:, None],
        "w_num": np.repeat(a["W_num"], J, axis=0),
        "b_num": np.repeat(a["b_num"], J, axis=0),
        "tables": a["cat_tables"],
        "wq": a["W_Q"],
        "wk": a["W_K"],
        "wv": a["W_V"],
        "wo_t": a["W_O"].transpose(0, 2, 1),
        "wres_t": a["W_Res"][:L - 1].transpose(0, 2, 1),
        "wres_last": a["W_Res"][L - 1],
        "w_fin": np.concatenate([fin[NUM_NUM:], fin[:NUM_NUM]]).T,
        "b_fin": np.repeat(a["b_final"][None], R * T, axis=0),
    }
    nc = bacc.Bacc("TRN2", target_bir_lowering=False, num_devices=1)
    arrays, args = {}, []
    for name, x in laid.items():
        x = np.ascontiguousarray(x)
        arrays[f"in_{name}"] = x
        args.append(nc.dram_tensor(f"in_{name}", x.shape, mybir.dt.from_np(x.dtype), kind="ExternalInput").ap())
    args.append(nc.dram_tensor("out_y", (R * T, STEPS), F32, kind="ExternalOutput").ap())
    recsys_attention(nc, *args)
    r = run(nc, [arrays], core_ids=[0])
    got = np.asarray(r.results[0]["out_y"]).reshape(G, J, T, STEPS)[..., LAG:]
    return np.ascontiguousarray(got.transpose(3, 0, 2, 1).reshape(-1)[:B])
```
